# Optimizing a Trainium2 kernel written in Bass

```python
import numpy as np
import jax
import jax.numpy as jnp

def _softmax(x, axis=-1):
    return jax.nn.softmax(x, axis=axis)

def _gelu(x):
    return jax.nn.gelu(x, approximate=True)

def _silu(x):
    return jax.nn.silu(x)

def _sigmoid(x):
    return jax.nn.sigmoid(x)

def _layernorm(x, axis=-1, eps=1e-05):
    m = jnp.mean(x, axis=axis, keepdims=True)
    v = jnp.var(x, axis=axis, keepdims=True)
    return (x - m) / jnp.sqrt(v + eps)

def _scatter_add(tgt, idx, src, axis=0):
    return tgt.at[idx].add(src)

def _segment_sum(src, seg, n):
    return jax.ops.segment_sum(src, seg, n)
kernel_name = 'mk_gnn_preln_d4_gnn_r8_3f3adc'

def setup_inputs(seed: int=0):
    np.random.seed(seed)
    _w = jnp.asarray

    def _rec_inputs():
        import jax
        import jax.numpy as jnp
        _gk = jax.random.key(seed)
        x = -0.000202 + 1 * jax.random.normal(jax.random.fold_in(_gk, 1), (6250, 64), jnp.float32)
        _s = jax.random.randint(jax.random.fold_in(_gk, 2), (100000,), 0, 6250, jnp.int32)
        _d = jax.random.randint(jax.random.fold_in(_gk, 3), (100000,), 0, 6250, jnp.int32)
        _loop = jnp.arange(6250, dtype=jnp.int32)
        src = jnp.concatenate([_s, _d, _loop])
        dst = jnp.concatenate([_d, _s, _loop])
        _o = jnp.argsort(dst, stable=True)
        src = src[_o]
        dst = dst[_o]
        edge_attr_64 = 0.000189758 + 1.00013 * jax.random.normal(jax.random.fold_in(_gk, 11), (206250, 64), jnp.float32)
        return (x, src, dst, edge_attr_64)
    x, src, dst, edge_attr_64 = _rec_inputs()

    def _L0_gnn_setup():
        import jax, jax.numpy as jnp
        import numpy as np
        N_NODES = 12500

        def gcn_conv(x, edge_index, W, b):
            n = x.shape[0]
            loops = jnp.arange(n, dtype=edge_index.dtype)
            row = jnp.concatenate([edge_index[0], loops])
            col = jnp.concatenate([edge_index[1], loops])
            deg = jax.ops.segment_sum(jnp.ones_like(col, dtype=x.dtype), col, num_segments=n)
            dinv = jnp.where(deg > 0, jax.lax.rsqrt(deg), 0.0)
            norm = dinv[row] * dinv[col]
            h = x @ W
            msg = h[row] * norm[:, None]
            out = jax.ops.segment_sum(msg, col, num_segments=n)
            return out + b
        key = jax.random.key(seed)
        ks = jax.random.split(key, 6)
        d_in, d_hid, d_out = (64, 64, 64)
        x = jax.random.normal(ks[0], (N_NODES, d_in), dtype=jnp.float32)
        edge_index = jax.random.randint(ks[1], (2, 400000), 0, N_NODES, dtype=jnp.int64)
        W1 = jax.random.normal(ks[2], (d_in, d_hid), dtype=jnp.float32) / np.sqrt(d_in)
        b1 = jax.random.normal(ks[3], (d_hid,), dtype=jnp.float32) * 0.01
        W2 = jax.random.normal(ks[4], (d_hid, d_out), dtype=jnp.float32) / np.sqrt(d_hid)
        b2 = jax.random.normal(ks[5], (d_out,), dtype=jnp.float32) * 0.01
        return {'x': x, 'edge_index': edge_index, 'W1': W1, 'b1': b1, 'W2': W2, 'b2': b2}
    _L0_gnn_all = _L0_gnn_setup()
    _L0_gnn_in = {k: v for k, v in _L0_gnn_all.items() if k in ('W1', 'b1', 'W2', 'b2')}
    del _L0_gnn_all

    def _L1_gnn_setup():
        import jax, jax.numpy as jnp
        import numpy as np
        N_NODES = 12500
        N_EDGES = 200000
        EMB_DIM = 64
        key = jax.random.key(seed)
        k1, k2, k3, k4, k5, k6 = jax.random.split(key, 6)
        x = jax.random.normal(k1, (N_NODES, EMB_DIM), dtype=jnp.float32)
        edge_index = jax.random.randint(k2, (2, N_EDGES), 0, N_NODES, dtype=jnp.int64)
        scale = 1.0 / np.sqrt(EMB_DIM)
        W1 = jax.random.normal(k3, (EMB_DIM, EMB_DIM), dtype=jnp.float32) * scale
        b1 = jax.random.normal(k4, (EMB_DIM,), dtype=jnp.float32) * scale
        W2 = jax.random.normal(k5, (EMB_DIM, EMB_DIM), dtype=jnp.float32) * scale
        b2 = jax.random.normal(k6, (EMB_DIM,), dtype=jnp.float32) * scale
        return {'x': x, 'edge_index': edge_index, 'W1': W1, 'b1': b1, 'W2': W2, 'b2': b2}
    _L1_gnn_all = _L1_gnn_setup()
    _L1_gnn_in = {k: v for k, v in _L1_gnn_all.items() if k in ('W1', 'b1', 'W2', 'b2')}
    del _L1_gnn_all

    def _L2_gnn_setup():
        import jax, jax.numpy as jnp
        import numpy as np
        N, E = (12500, 200000)
        DIM, H, D = (64, 4, 8)
        DH = D * H
        QK_SCALE = (DIM // H) ** (-0.5)
        key = jax.random.key(seed)
        k1, k2, k3, k4 = jax.random.split(key, 4)
        x = jax.random.normal(k1, (N, DIM), dtype=jnp.float32)
        edge_index = jax.random.randint(k2, (2, E), 0, N, dtype=jnp.int64)
        W_qkv = jax.random.normal(k3, (DIM, 2 * DH + DIM), dtype=jnp.float32) * DIM ** (-0.5)
        b_qkv = jax.random.normal(k4, (2 * DH + DIM,), dtype=jnp.float32) * 0.02
        return {'x': x, 'edge_index': edge_index, 'W_qkv': W_qkv, 'b_qkv': b_qkv}
    _L2_gnn_all = _L2_gnn_setup()
    _L2_gnn_in = {k: v for k, v in _L2_gnn_all.items() if k in ('W_qkv', 'b_qkv')}
    del _L2_gnn_all

    def _L3_gnn_setup():
        import jax, jax.numpy as jnp
        import numpy as np
        N_NODES = 6250
        N_EDGES = 100000
        D = 64
        EPS = 0.0
        key = jax.random.key(seed)
        ks = jax.random.split(key, 10)
        x = jax.random.normal(ks[0], (N_NODES, D), dtype=jnp.float32)
        edge_index = jax.random.randint(ks[1], (2, N_EDGES), 0, N_NODES, dtype=jnp.int64)
        edge_attr = jax.random.normal(ks[2], (N_EDGES, D), dtype=jnp.float32)
        s = 1.0 / np.sqrt(D)
        W1 = jax.random.uniform(ks[3], (D, D), jnp.float32, -s, s)
        b1 = jax.random.uniform(ks[4], (D,), jnp.float32, -s, s)
        W2 = jax.random.uniform(ks[5], (D, D), jnp.float32, -s, s)
        b2 = jax.random.uniform(ks[6], (D,), jnp.float32, -s, s)
        W3 = jax.random.uniform(ks[7], (D, D), jnp.float32, -s, s)
        b3 = jax.random.uniform(ks[8], (D,), jnp.float32, -s, s)
        return {'x': x, 'edge_index': edge_index, 'edge_attr': edge_attr, 'W1': W1, 'b1': b1, 'W2': W2, 'b2': b2, 'W3': W3, 'b3': b3}
    _L3_gnn_all = _L3_gnn_setup()
    _L3_gnn_in = {k: v for k, v in _L3_gnn_all.items() if k in ('W1', 'b1', 'W2', 'b2', 'W3', 'b3')}
    del _L3_gnn_all
    return {'x': x, 'src': src, 'dst': dst, 'edge_attr_64': edge_attr_64, 'L0_gnn_W1': _L0_gnn_in['W1'], 'L0_gnn_b1': _L0_gnn_in['b1'], 'L0_gnn_W2': _L0_gnn_in['W2'], 'L0_gnn_b2': _L0_gnn_in['b2'], 'L1_gnn_W1': _L1_gnn_in['W1'], 'L1_gnn_b1': _L1_gnn_in['b1'], 'L1_gnn_W2': _L1_gnn_in['W2'], 'L1_gnn_b2': _L1_gnn_in['b2'], 'L2_gnn_W_qkv': _L2_gnn_in['W_qkv'], 'L2_gnn_b_qkv': _L2_gnn_in['b_qkv'], 'L3_gnn_W1': _L3_gnn_in['W1'], 'L3_gnn_b1': _L3_gnn_in['b1'], 'L3_gnn_W2': _L3_gnn_in['W2'], 'L3_gnn_b2': _L3_gnn_in['b2'], 'L3_gnn_W3': _L3_gnn_in['W3'], 'L3_gnn_b3': _L3_gnn_in['b3']}

def reference(x, src, dst, edge_attr_64, L0_gnn_W1, L0_gnn_b1, L0_gnn_W2, L0_gnn_b2, L1_gnn_W1, L1_gnn_b1, L1_gnn_W2, L1_gnn_b2, L2_gnn_W_qkv, L2_gnn_b_qkv, L3_gnn_W1, L3_gnn_b1, L3_gnn_W2, L3_gnn_b2, L3_gnn_W3, L3_gnn_b3):
    import jax
    import jax.numpy as jnp

    def _L0_gnn_ref(x, edge_index, W1, b1, W2, b2):
        import jax, jax.numpy as jnp
        import numpy as np
        N_NODES = 12500

        def gcn_conv(x, edge_index, W, b):
            n = x.shape[0]
            loops = jnp.arange(n, dtype=edge_index.dtype)
            row = jnp.concatenate([edge_index[0], loops])
            col = jnp.concatenate([edge_index[1], loops])
            deg = jax.ops.segment_sum(jnp.ones_like(col, dtype=x.dtype), col, num_segments=n)
            dinv = jnp.where(deg > 0, jax.lax.rsqrt(deg), 0.0)
            norm = dinv[row] * dinv[col]
            h = x @ W
            msg = h[row] * norm[:, None]
            out = jax.ops.segment_sum(msg, col, num_segments=n)
            return out + b
        h = jax.nn.relu(gcn_conv(x, edge_index, W1, b1))
        out = jax.nn.relu(gcn_conv(h, edge_index, W2, b2))
        return out

    def _L1_gnn_ref(x, edge_index, W1, b1, W2, b2):
        import jax, jax.numpy as jnp
        import numpy as np
        N_NODES = 12500
        N_EDGES = 200000
        EMB_DIM = 64
        row, col = (edge_index[0], edge_index[1])
        n = x.shape[0]
        deg = jax.ops.segment_sum(jnp.ones_like(col, dtype=x.dtype), col, num_segments=n)
        deg_inv_sqrt = jnp.where(deg > 0, jax.lax.rsqrt(jnp.maximum(deg, 1.0)), 0.0)
        norm = deg_inv_sqrt[row] * deg_inv_sqrt[col]
        xr = x[row]
        xc = x[col]
        msg = norm[:, None] * (xc @ W1.T + b1 + xr * xc @ W2.T + b2)
        agg = jax.ops.segment_sum(msg, row, num_segments=n)
        return jax.nn.leaky_relu(agg, negative_slope=0.2)

    def _L2_gnn_ref(x, edge_index, W_qkv, b_qkv):
        import jax, jax.numpy as jnp
        import numpy as np
        N, E = (12500, 200000)
        DIM, H, D = (64, 4, 8)
        DH = D * H
        QK_SCALE = (DIM // H) ** (-0.5)
        n = x.shape[0]
        e = edge_index.shape[1]
        qkv = x @ W_qkv + b_qkv
        q = qkv[:, :DH].reshape(n, H, D)
        k = qkv[:, DH:2 * DH].reshape(n, H, D)
        v = qkv[:, 2 * DH:].reshape(n, H, DIM // H)
        s, t = (edge_index[0], edge_index[1])
        q_e = q[s] * QK_SCALE
        k_e = k[t]
        v_e = v[t]
        deg = jax.ops.segment_sum(jnp.ones((e,), x.dtype), s, num_segments=n)
        q_e = q_e * (deg[s] ** (-0.5))[:, None, None]
        compat = jnp.einsum('ehd,ehd->eh', q_e, k_e)
        m = jax.ops.segment_max(compat, s, num_segments=n)
        ex = jnp.exp(compat - m[s])
        denom = jax.ops.segment_sum(ex, s, num_segments=n)
        attn = ex / (denom[s] + 1e-16)
        msg = (v_e * attn[..., None]).reshape(e, DIM)
        out = jax.ops.segment_sum(msg, s, num_segments=n)
        return out

    def _L3_gnn_ref(x, edge_index, edge_attr, W1, b1, W2, b2, W3, b3):
        import jax, jax.numpy as jnp
        import numpy as np
        N_NODES = 6250
        N_EDGES = 100000
        D = 64
        EPS = 0.0
        src = edge_index[0]
        dst = edge_index[1]
        msg = jax.nn.relu(x[src] + edge_attr)
        aggr = jax.ops.segment_sum(msg, dst, num_segments=x.shape[0])
        h = (1.0 + EPS) * x + aggr
        h = jax.nn.relu(h @ W1.T + b1)
        h = jax.nn.relu(h @ W2.T + b2)
        return h @ W3.T + b3
    edge_index = jnp.stack([src, dst])
    h = jnp.maximum(_layernorm(x, axis=-1), 0.0)
    x = x + _L0_gnn_ref(h, edge_index, L0_gnn_W1, L0_gnn_b1, L0_gnn_W2, L0_gnn_b2)
    h = jnp.maximum(_layernorm(x, axis=-1), 0.0)
    x = x + _L1_gnn_ref(h, edge_index, L1_gnn_W1, L1_gnn_b1, L1_gnn_W2, L1_gnn_b2)
    h = jnp.maximum(_layernorm(x, axis=-1), 0.0)
    x = x + _L2_gnn_ref(h, edge_index, L2_gnn_W_qkv, L2_gnn_b_qkv)
    h = jnp.maximum(_layernorm(x, axis=-1), 0.0)
    x = x + _L3_gnn_ref(h, edge_index, edge_attr_64, L3_gnn_W1, L3_gnn_b1, L3_gnn_W2, L3_gnn_b2, L3_gnn_W3, L3_gnn_b3)
    return x

_drawn_inputs = setup_inputs


def setup_inputs(seed=0):
    import zlib

    import numpy as np

    out = dict(_drawn_inputs(seed))
    spreads = {}
    factors = {'L0_gnn_b1': 8.0,
     'L0_gnn_b2': 8.0,
     'L2_gnn_b_qkv': 5.085,
     'L3_gnn_b1': 8.0,
     'L3_gnn_b2': 3.886}
    for name, (base, spread) in spreads.items():
        noise = np.random.default_rng([zlib.crc32(name.encode()), seed]).standard_normal(out[name].shape)
        drawn = base * np.exp(spread * noise) if base else spread * noise
        out[name] = jnp.asarray(drawn.astype(out[name].dtype))
    for name, factor in factors.items():
        out[name] = (out[name] * factor).astype(out[name].dtype)
    return out
```

```python
import concourse.bass as bass
from concourse import mybir
from contextlib import ExitStack

F32 = mybir.dt.float32
BF16 = mybir.dt.bfloat16
I32 = mybir.dt.int32
ALU = mybir.AluOpType
ACT = mybir.ActivationFunctionType
AX_X = mybir.AxisListType.X

P = 128
N_NODES, D = 6250, 64
N_EDGES = 206250
CH = -(-N_NODES // P)
TAIL = N_NODES - (CH - 1) * P
EP = 125
ET = N_EDGES // EP
GROUP = 5
DIAG = 4
SLOTS = CH + DIAG - 1
MAIN = CH * SLOTS
NT = MAIN + ET + 1
BT = 4
NB = SLOTS // BT
H, DH, DV = 4, 8, 16
QK_SCALE = float(D // H) ** -0.5
BIG = 1.0e30
PARTS = 6
QS = PARTS * DH
assert EP * ET == N_EDGES and NB * BT == SLOTS and ET % (2 * GROUP) == 0

SRC, DST = 0, 1


class Kernel:
    pass


def counted(eng, sem):
    n = [0]

    def link(ins):
        n[0] += 1
        ins.then_inc(sem, 1)
        eng.wait_ge(sem, n[0])

    return link


def end_phase(nc, sems):
    for s in sems:
        nc.gpsimd.sem_clear(s)
    nc.all_engine_barrier()


class Phase:

    def __init__(self, nc, name):
        self.nc, self.name, self.sems, self.starts, self.ctx = nc, f"p{nc.next_id()}_{name}", [], [], ExitStack()

    def __enter__(self):
        self.ctx.__enter__()
        return self

    def sem(self, name, start=0):
        s = self.ctx.enter_context(self.nc.semaphore(f"{self.name}_{name}"))
        self.sems.append(s)
        if start:
            self.starts.append((s, start))
        return s

    def begin(self):
        for s, start in self.starts:
            self.nc.gpsimd.sem_inc(s, start)
        self.nc.all_engine_barrier()

    def sb(self, name, shape, dt):
        return self.ctx.enter_context(self.nc.sbuf_tensor(f"{self.name}_{name}", shape, dt))

    def ps(self, name, shape, dt):
        return self.ctx.enter_context(self.nc.psum_tensor(f"{self.name}_{name}", shape, dt))

    def __exit__(self, *a):
        if a[0] is None:
            end_phase(self.nc, self.sems)
        return self.ctx.__exit__(*a)


def bcast_mid(ap, n):
    return ap.unsqueeze(1).to_broadcast([ap.shape[0], n, ap.shape[1]])


def bcast_last(ap, n):
    return ap.unsqueeze(2).to_broadcast([ap.shape[0], ap.shape[1], n])


def setup_phase(nc, k):
    with Phase(nc, "setup") as ph:
        made, loaded, filled = ph.sem("made"), ph.sem("loaded"), ph.sem("filled")
        conv = ph.sem("converted")
        idn = ph.sem("identity")
        blank = ph.sb("blank", [P, 2 * NT], F32)
        ioti = ph.sb("ioti", [P, P], I32)
        slot_row = ph.sb("slot_row", [P, 1], I32)
        with nc.Block() as block:

            @block.gpsimd
            def _(eng):
                eng.iota(ioti[:], pattern=[[1, P]], base=0, channel_multiplier=0).then_inc(made, 1)
                eng.iota(slot_row[:], pattern=[[0, 1]], base=MAIN, channel_multiplier=NT).then_inc(made, 1)
                eng.memset(k.ident[:], 0.0).then_inc(idn, 1)
                eng.memset(k.identb[:], 0.0).then_inc(idn, 1)
                eng.memset(k.later[:], 1.0).then_inc(idn, 1)
                eng.memset(k.neg_ident[:], 0.0).then_inc(idn, 1)
                eng.wait_ge(idn, 4)
                for m, fill in ((k.ident, 1.0), (k.identb, 1.0), (k.neg_ident, -BIG)):
                    eng.affine_select(out=m[:], in_=m[:], compare_op=ALU.not_equal, fill=fill, base=0,
                                      pattern=[[-1, P]], channel_multiplier=1).then_inc(idn, 1)
                eng.affine_select(out=k.later[:], in_=k.later[:], compare_op=ALU.is_gt, fill=0.0, base=0,
                                  pattern=[[-1, EP]], channel_multiplier=1).then_inc(idn, 1)
                eng.wait_ge(idn, 8)
                eng.wait_ge(conv, 1)
                for b in range(2):
                    half = slice(b * P // 2, (b + 1) * P // 2)
                    eng.dma_start(k.edge_meta.rearrange("(p t) c -> p (t c)", p=P)[half, :], blank[half, :])\
                       .then_inc(k.sent[b], 16)
                for b in range(2):
                    eng.wait_ge(k.sent[b], 16)

            @block.vector
            def _(eng):
                eng.memset(blank[:], -1.0e6).then_inc(conv, 1)
                eng.memset(k.X[:], 0.0).then_inc(conv, 1)
                eng.wait_ge(made, 2)
                eng.tensor_copy(k.iota[:], ioti[:]).then_inc(conv, 1)
                eng.tensor_copy(k.slot_row[:], slot_row[:]).then_inc(conv, 1)
                eng.wait_ge(conv, 4)

            @block.sync
            def _(eng):
                eng.wait_ge(conv, 2)
                for a, b in ((0, CH // 2), (CH // 2, CH - 1)):
                    eng.dma_start(k.X[:, a:b, :], k.x[a * P:b * P, :].rearrange("(c p) d -> p c d", p=P))\
                       .then_inc(loaded, 16)
                eng.dma_start(k.X[0:TAIL, CH - 1, :], k.x[(CH - 1) * P:N_NODES, :]).then_inc(loaded, 16)
                for dst, w in k.weights:
                    eng.dma_start(dst, w).then_inc(loaded, 16)
                attr = k.edge_rows.rearrange("(p t) c -> p (t c)", p=P)
                for c in range(D // 2):
                    eng.dma_start(attr[:, c * 2 * NT:(c + 1) * 2 * NT], blank[:]).then_inc(filled, 16)
                eng.wait_ge(filled, 16 * (D // 2))
                eng.wait_ge(loaded, 16 * (3 + len(k.weights)))


def place_phase(nc, k):
    with Phase(nc, "place") as ph:
        ends = ph.sb("ends", [EP, 2, ET], I32)
        local = ph.sb("local", [EP, 2, ET], F32)
        chunk = ph.sb("chunk", [EP, 2, ET], F32)
        whole = ph.sb("whole", [EP, 2, ET], F32)
        tmpi = ph.sb("tmpi", [EP, 2, ET], I32)
        hot_c = [ph.sb(f"hot_chunk{i}", [EP, GROUP, 2, CH], BF16) for i in range(2)]
        hot_l = [ph.sb(f"hot_local{i}", [EP, GROUP, 2, P], BF16) for i in range(2)]
        hot_t = [ph.sb(f"hot_t{i}", [2 * CH, GROUP, EP], BF16) for i in range(2)]
        cum_hi, cum_lo = ph.sb("cum_hi", [CH, CH], BF16), ph.sb("cum_lo", [CH, CH], BF16)
        zero = ph.sb("zero", [EP, P], BF16)
        junk = ph.sb("junk", [EP, GROUP, P], F32)
        junk2 = ph.sb("junk2", [EP, GROUP, CH], F32)
        rin, rbe = ph.sb("rank_in_tile", [EP, GROUP], F32), ph.sb("rank_before", [EP, GROUP], F32)
        t = ph.sb("t", [EP, 12, GROUP], F32)
        scan = ph.sb("scan", [EP, 4, 4 + GROUP], F32)
        spilled = ph.sb("spilled", [EP, 1], F32)
        spill_row = ph.sb("spill_row", [1, 2], F32)
        index = [ph.sb(f"index{i}", [EP, GROUP], I32) for i in range(2)]
        meta = [ph.sb(f"meta{i}", [EP, GROUP, 2], F32) for i in range(2)]
        rows = [ph.sb(f"rows{i}", [EP, GROUP, D], F32) for i in range(2)]
        psT = [ph.ps(f"psT{i}", [2 * CH, GROUP, P], BF16) for i in range(2)]
        psS = ph.ps("same", [EP, 2 * 4, P], F32)
        psG = ph.ps("before", [EP, 512], F32)
        psC = ph.ps("counts", [CH, 512], F32)
        psD = ph.ps("degrees", [P, 512], F32)
        loaded, done = ph.sem("loaded"), ph.sem("converted")
        hot_ready, t_ready, t_copied = ph.sem("hot_ready"), ph.sem("t_ready"), ph.sem("t_copied")
        same_ready, count_ready, cum_ready = ph.sem("same_ready"), ph.sem("count_ready"), ph.sem("cum_ready", 1)
        ranked, idx_ready = ph.sem("ranked", 1), ph.sem("idx_ready")
        rows_in = [ph.sem(f"rows_in{i}") for i in range(2)]
        sent = k.sent
        chain = ph.sem("chain")
        fin, sending = ph.sem("fin"), ph.sem("sending")
        groups = ET // GROUP
        ph.begin()
        edge_rows = k.edge_attr.rearrange("(p t) d -> p t d", p=EP)
        with nc.Block() as block:

            @block.sync
            def _(eng):
                for w, a in ((SRC, k.src), (DST, k.dst)):
                    eng.dma_start(ends[:, w, :], a.rearrange("(p t) -> p t", p=EP)).then_inc(loaded, 16)
                with eng.Fori(0, groups // 2) as i:
                    for b in range(2):
                        eng.wait_ge(sent[b], i * (GROUP * 32) + 16)
                        eng.dma_start(rows[b][:], edge_rows[:, bass.ds((2 * i + b) * GROUP, GROUP), :])\
                           .then_inc(rows_in[b], 16)

            @block.gpsimd
            def _(eng):
                last_row = eng.alloc_register("last_row")
                eng.reg_mov(last_row, P * NT - 1)
                with eng.Fori(0, groups // 2) as i:
                    for b in range(2):
                        placed, brought = eng.snap(2 * i + b + 1), eng.snap(16 * i + 16)
                        eng.wait_ge(idx_ready, placed)
                        eng.wait_ge(rows_in[b], brought)
                        eng.sem_inc(sending, 1)
                        for j in range(GROUP):
                            at = bass.IndirectOffsetOnAxis(index[b][:, j:j + 1], 0)
                            eng.indirect_dma_start(k.edge_meta, at, meta[b][:, j, :], None,
                                                   bounds_check=last_row, oob_is_err=False).then_inc(sent[b], 16)
                            eng.indirect_dma_start(k.edge_rows, at, rows[b][:, j, :], None,
                                                   bounds_check=last_row, oob_is_err=False).then_inc(sent[b], 16)
                for b in range(2):
                    eng.wait_ge(sent[b], 16 + 32 * GROUP * (groups // 2))

            @block.vector
            def _(eng):
                link = counted(eng, done)
                eng.memset(zero[:], 0.0)
                eng.memset(spilled[:], 0.0)
                eng.memset(cum_hi[:], 0.0)
                eng.memset(cum_lo[:], 0.0)
                link(eng.memset(scan[:], 0.0))
                eng.wait_ge(loaded, 32)
                link(eng.tensor_single_scalar(tmpi[:], ends[:], 7, ALU.arith_shift_right))
                link(eng.tensor_copy(chunk[:], tmpi[:]))
                link(eng.tensor_copy(whole[:], ends[:]))
                link(eng.scalar_tensor_tensor(local[:], chunk[:], -float(P), whole[:], ALU.mult, ALU.add))

                def clink(n, ins):
                    ins.then_inc(chain, 1)
                    eng.wait_ge(chain, n)

                with eng.Fori(0, groups // 2) as i:
                    for b in range(2):
                        g = 2 * i + b
                        steps = [0]

                        def step(ins, g=g, steps=steps):
                            steps[0] += 1
                            clink(g * CHAIN + steps[0], ins)

                        at = bass.ds(g * GROUP, GROUP)
                        for w in (SRC, DST):
                            eng.tensor_tensor(hot_c[b][:, :, w, :], bcast_mid(k.iota[0:EP, 0:CH], GROUP),
                                              bcast_last(chunk[:, w, at], CH), ALU.is_equal).then_inc(hot_ready, 1)
                            eng.tensor_tensor(hot_l[b][:, :, w, :], bcast_mid(k.iota[0:EP, :], GROUP),
                                              bcast_last(local[:, w, at], P), ALU.is_equal).then_inc(hot_ready, 1)
                        step(eng.tensor_tensor(t[:, 0, :], chunk[:, SRC, at], chunk[:, DST, at], ALU.is_equal))
                        for j in range(GROUP):
                            eng.wait_ge(count_ready, g * GROUP + j + 1)
                            step(eng.tensor_scalar(cum_hi[:], psC[:, 0:CH], 32000.0, None, ALU.min))
                            eng.scalar_tensor_tensor(cum_lo[:], psC[:, 0:CH], 32000.0, cum_hi[:], ALU.min,
                                                     ALU.subtract).then_inc(cum_ready, 1)
                            if j == 0:
                                eng.wait_ge(same_ready, g + 1)
                            eng.scalar_tensor_tensor(junk[:, j, 0:EP], psS[:, j, 0:EP], 1.5, k.later[0:EP, :],
                                                     ALU.is_gt, ALU.mult, accum_out=rin[:, j:j + 1])
                        step(eng.tensor_tensor(junk2[:], psG[:, 0:GROUP * CH].rearrange("p (t c) -> p t c", c=CH),
                                               hot_c[b][:, :, DST, :], ALU.mult))
                        eng.tensor_reduce(rbe[:], junk2[:], AX_X, ALU.add).then_inc(ranked, 1)
                        eng.wait_ge(ranked, g + 2)
                        r, m1, m, q, e = (t[:, n, :] for n in (1, 2, 3, 4, 0))
                        step(eng.tensor_tensor(r, rin[:], rbe[:], ALU.add))
                        step(eng.tensor_single_scalar(m1, r, 128.0, ALU.is_ge))
                        step(eng.scalar_tensor_tensor(m, r, 256.0, m1, ALU.is_ge, ALU.add))
                        step(eng.scalar_tensor_tensor(t[:, 5, :], r, 384.0, m, ALU.is_ge, ALU.add))
                        m = t[:, 5, :]
                        step(eng.tensor_tensor(t[:, 6, :], m1, e, ALU.is_gt))
                        step(eng.scalar_tensor_tensor(scan[:, 0, 4:], r, 128.0 * DIAG, t[:, 6, :], ALU.is_ge, ALU.max))
                        for n, s in ((0, 1), (1, 2), (2, 4)):
                            step(eng.tensor_tensor(scan[:, n + 1, 4:], scan[:, n, 4:],
                                                   scan[:, n, 4 - s:4 - s + GROUP], ALU.add))
                        step(eng.tensor_scalar(t[:, 7, :], scan[:, 3, 4:], spilled[:], k.slot_row[0:EP, :],
                                               ALU.add, ALU.add))
                        step(eng.tensor_tensor(t[:, 8, :], t[:, 7, :], scan[:, 0, 4:], ALU.subtract))
                        step(eng.tensor_tensor(spilled[:], spilled[:], scan[:, 3, 3 + GROUP:4 + GROUP], ALU.add))
                        step(eng.scalar_tensor_tensor(t[:, 9, :], m, float(CH - 1), chunk[:, SRC, at], ALU.add,
                                                      ALU.subtract))
                        step(eng.tensor_tensor(t[:, 10, :], t[:, 9, :], m1, ALU.mult))
                        step(eng.tensor_tensor(t[:, 11, :], t[:, 10, :], chunk[:, SRC, at], ALU.add))
                        step(eng.scalar_tensor_tensor(t[:, 9, :], chunk[:, DST, at], float(SLOTS), t[:, 11, :],
                                                      ALU.mult, ALU.add))
                        step(eng.scalar_tensor_tensor(q, m, -128.0, r, ALU.mult, ALU.add))
                        step(eng.scalar_tensor_tensor(t[:, 10, :], q, float(NT), t[:, 9, :], ALU.mult, ALU.add))
                        step(eng.tensor_tensor(t[:, 11, :], t[:, 8, :], t[:, 10, :], ALU.subtract))
                        step(eng.tensor_tensor(t[:, 6, :], t[:, 11, :], scan[:, 0, 4:], ALU.mult))
                        eng.wait_ge(sent[b], i * (GROUP * 32) + 16)
                        step(eng.tensor_copy(meta[b][:].rearrange("p t w -> p w t"), whole[:, :, at]))
                        eng.tensor_tensor(index[b][:], t[:, 6, :], t[:, 10, :], ALU.add).then_inc(idx_ready, 1)
                        assert steps[0] == CHAIN
                eng.tensor_copy(k.deg[:, SRC, :], psD[:, 0:CH])
                eng.tensor_copy(k.deg[:, DST, :], psD[:, CH:2 * CH])
                eng.wait_ge(fin, 2)
                eng.tensor_reduce(spill_row[0:1, 0:1], psC[0:1, 0:EP], AX_X, ALU.max).then_inc(fin, 1)
                eng.wait_ge(fin, 3)
                eng.tensor_scalar(k.rounds[:], spill_row[0:1, 0:1], 1.0, None, ALU.add).then_inc(fin, 1)
                eng.wait_ge(fin, 4)

            @block.scalar
            def _(eng):
                with eng.Fori(0, groups // 2) as i:
                    for b in range(2):
                        g = 2 * i + b
                        eng.wait_ge(t_ready, g + 1)
                        eng.copy(hot_t[b][:], psT[b][:, :, 0:EP])\
                           .then_inc(t_copied, 1)

            @block.tensor
            def _(eng):
                eng.wait_ge(done, 1)
                eng.matmul(psC[:, 0:CH], zero[:, 0:CH], zero[:, 0:CH], start=True, stop=True)
                eng.matmul(psD[:, 0:2 * CH], zero[:, :], zero[:, 0:2 * CH], start=True, stop=True)
                with eng.Fori(0, groups // 2) as i:
                    for b in range(2):
                        g = 2 * i + b
                        eng.wait_ge(hot_ready, 4 * g + 4)
                        for j in range(GROUP):
                            last = eng.transpose(psT[b][:, j, 0:EP],
                                                 hot_c[b][:, j, :, :].rearrange("p w c -> p (w c)"),
                                                 k.identb[0:EP, 0:EP])
                        last.then_inc(t_ready, 1)
                        for j in range(GROUP):
                            for w in (SRC, DST):
                                eng.matmul(psD[:, w * CH:(w + 1) * CH], hot_l[b][:, j, w, :], hot_c[b][:, j, w, :],
                                           start=False, stop=True, skip_group_check=True)
                        eng.wait_ge(t_copied, g + 1)
                        eng.wait_ge(ranked, g + 1)
                        for j in range(GROUP):
                            last = eng.matmul(psS[:, j, 0:EP], hot_t[b][:, j, :], hot_t[b][:, j, :],
                                              start=True, stop=True)
                        last.then_inc(same_ready, 1)
                        for j in range(GROUP):
                            eng.wait_ge(cum_ready, g * GROUP + (j + 1))
                            before = psG[:, j * CH:(j + 1) * CH]
                            eng.matmul(before, hot_t[b][0:CH, j, :], cum_hi[:], start=True, stop=False)
                            eng.matmul(before, hot_t[b][0:CH, j, :], cum_lo[:], start=False, stop=True)
                            eng.matmul(psC[:, 0:CH], hot_c[b][:, j, SRC, :], hot_c[b][:, j, DST, :],
                                       start=False, stop=True, skip_group_check=True).then_inc(count_ready, 1)
                eng.wait_ge(chain, groups * CHAIN)
                eng.wait_ge(cum_ready, groups * GROUP + 1)
                eng.matmul(psC[0:1, 0:EP], spilled[:], k.ident[0:EP, 0:EP], start=True, stop=True).then_inc(fin, 2)


CHAIN = 1 + GROUP + 22


def tiles_phase(nc, k, tile):
    with Phase(nc, "tiles" if tile is None else "spill_tiles") as ph:
        raw = ph.sb("raw", [P, CH, SLOTS, 2] if tile is None else [P, 1, 1, 2], F32)
        loaded, made = ph.sem("loaded"), ph.sem("made")
        ph.begin()
        meta = k.edge_meta.rearrange("(p t) c -> p t c", p=P)
        with nc.Block() as block:

            @block.sync
            def _(eng):
                if tile is None:
                    eng.dma_start(raw[:], meta[:, 0:MAIN, :].rearrange("p (j s) c -> p j s c", s=SLOTS))\
                       .then_inc(loaded, 16)
                else:
                    eng.dma_start(raw[:, 0, :, :], meta[:, bass.ds(tile, 1), :]).then_inc(loaded, 16)
                eng.wait_ge(loaded, 16)

            @block.vector
            def _(eng):
                link = counted(eng, made)

                def ends(w, a, b):
                    if tile is None:
                        return raw[:, :, a:b, w]
                    return raw[:, :, :, w].to_broadcast([P, CH, b - a])

                chunks = k.iota[:, 0:CH]
                eng.wait_ge(loaded, 16)
                link(eng.scalar_tensor_tensor(k.by_dst[:, SRC, :, 0:CH], bcast_mid(chunks, CH), -float(P),
                                              ends(SRC, 0, CH), ALU.mult, ALU.add))
                if tile is None:
                    link(eng.scalar_tensor_tensor(k.by_dst[:, SRC, :, CH:], bcast_last(chunks, DIAG - 1), -float(P),
                                                  ends(SRC, CH, SLOTS), ALU.mult, ALU.add))
                link(eng.scalar_tensor_tensor(k.by_dst[:, DST, :, :], bcast_last(chunks, SLOTS), -float(P),
                                              ends(DST, 0, SLOTS), ALU.mult, ALU.add))
                if tile is not None:
                    link(eng.memset(k.by_dst[:, :, :, CH:], -1.0))
                for w in (SRC, DST):
                    link(eng.tensor_copy(k.by_src[:, w, :, 0:CH], k.by_dst[:, w, :, 0:CH].rearrange("p j i -> p i j")))
                    link(eng.tensor_copy(k.by_src[:, w, :, CH:], k.by_dst[:, w, :, CH:]))


def in_rounds(nc, k, one_round):
    with nc.Fori(0, k.n_rounds) as rnd:
        one_round(rnd)
        with nc.If(k.n_rounds > 1):
            with nc.If(rnd + 1 < k.n_rounds):
                tiles_phase(nc, k, MAIN + rnd)
            with nc.Else():
                tiles_phase(nc, k, None)


def done(row, b):
    return row * NB + (NB + b + 1)


def chunk_of(row, b, j):
    s = b * BT + j
    return bass.ds(s, 1) if s < CH else bass.ds(row, 1)


def flat(ap):
    return ap.rearrange("p a b -> p (a b)")


def sum_phase(nc, k, name, frm, to, ends, table, width):
    with Phase(nc, name) as ph:
        hot = [ph.sb(f"hot{i}", [P, 2, BT, P], BF16) for i in range(3)]
        counts = [ph.sb(f"counts{i}", [P, BT, P], BF16) for i in range(3)]
        psA = [ph.ps(f"psA{i}", [P, BT * P], F32) for i in range(3)]
        acc = ph.ps("acc", [P, 512], F32)
        hot_ready, counted_, copied = ph.sem("hot_ready"), ph.sem("counted", NB), ph.sem("copied", NB)
        applied, row_read = ph.sem("applied", NB), ph.sem("row_read", 1)
        ph.begin()
        which = [2 if b == NB - 1 else b % 2 for b in range(NB)]
        with nc.Block() as block:

            @block.vector
            def _(eng):
                with eng.Fori(0, CH) as row:
                    for b in range(NB):
                        eng.wait_ge(counted_, done(row, b - 2))
                        for n, w in enumerate((frm, to)):
                            eng.tensor_tensor(hot[which[b]][:, n, :, :], bcast_mid(k.iota[:], BT),
                                              bcast_last(ends[:, w, bass.ds(row, 1), b * BT:(b + 1) * BT]
                                                         .rearrange("p a b -> p (a b)"), P),
                                              ALU.is_equal).then_inc(hot_ready, 1)
                    eng.wait_ge(applied, done(row, NB - 1))
                    here = k.sums[:, bass.ds(row, 1), 0:width].rearrange("p a b -> p (a b)")
                    eng.tensor_tensor(here, here, acc[:, 0:width], ALU.add).then_inc(row_read, 1)

            @block.scalar
            def _(eng):
                with eng.Fori(0, CH) as row:
                    for b in range(NB):
                        eng.wait_ge(counted_, done(row, b))
                        eng.wait_ge(applied, done(row, b - 2))
                        eng.copy(flat(counts[which[b]][:]), psA[which[b]][:]).then_inc(copied, 1)

            @block.tensor
            def _(eng):
                def apply(row, b):
                    eng.wait_ge(copied, done(row, b))
                    if b == 0:
                        eng.wait_ge(row_read, row + 1)
                    for j in range(BT):
                        inner = chunk_of(row, b, j)
                        for part in range(3):
                            last = eng.matmul(acc[:, 0:width], counts[which[b]][:, j, :],
                                              table[:, inner, part, 0:width].rearrange("p a b -> p (a b)"),
                                              start=(b == 0 and j == 0 and part == 0),
                                              stop=(b == NB - 1 and j == BT - 1 and part == 2))
                    last.then_inc(applied, 1)

                with eng.Fori(0, CH) as row:
                    for b in range(NB):
                        eng.wait_ge(hot_ready, row * (2 * NB) + (2 * b + 2))
                        eng.wait_ge(copied, done(row, b - 2))
                        for j in range(BT):
                            last = eng.matmul(psA[which[b]][:, j * P:(j + 1) * P], hot[which[b]][:, 0, j, :],
                                              hot[which[b]][:, 1, j, :], start=True, stop=True)
                        last.then_inc(counted_, 1)
                        if b:
                            apply(row, b - 1)
                    apply(row, NB - 1)


def max_phase(nc, k):
    with Phase(nc, "max") as ph:
        hot = [ph.sb(f"hot{i}", [P, 2, BT, P], BF16) for i in range(3)]
        none = [ph.sb(f"none{i}", [P, BT, P], BF16) for i in range(3)]
        query, own_key = ph.sb("query", [P, H // 2, P], BF16), ph.sb("own_key", [P, H // 2, P], BF16)
        tops = ph.sb("tops", [P, SLOTS, H // 2, 2], F32)
        top = ph.sb("top", [P, H], F32)
        psA = [ph.ps(f"psA{i}", [P, BT * P], F32) for i in range(3)]
        psS = [ph.ps(f"psS{i}", [P, H * P], F32) for i in range(4)]
        hot_ready, counted_, copied = ph.sem("hot_ready"), ph.sem("counted", NB), ph.sem("copied", NB)
        scored, read = ph.sem("scored", SLOTS), ph.sem("read", SLOTS)
        query_ready, row_done = ph.sem("query_ready"), ph.sem("row_done")
        ph.begin()
        which = [2 if b == NB - 1 else b % 2 for b in range(NB)]
        with nc.Block() as block:

            @block.vector
            def _(eng):
                def tops_of(row, b):
                    for n in range(BT):
                        s, odd = b * BT + n // 2 * 2, n % 2
                        eng.wait_ge(scored, row * SLOTS + (SLOTS + b * BT + n + 1))
                        eng.tensor_reduce(tops[:, s:s + 2, :, odd],
                                          psS[n][:].rearrange("p (s h t) -> p s h t", s=2, h=H // 2),
                                          AX_X, ALU.max).then_inc(read, 1)

                with eng.Fori(0, CH) as row:
                    for b in range(NB):
                        eng.wait_ge(counted_, done(row, b - 2))
                        for n, w in enumerate((SRC, DST)):
                            eng.tensor_tensor(hot[which[b]][:, n, :, :], bcast_mid(k.iota[:], BT),
                                              bcast_last(k.by_src[:, w, bass.ds(row, 1), b * BT:(b + 1) * BT]
                                                         .rearrange("p a b -> p (a b)"), P),
                                              ALU.is_equal).then_inc(hot_ready, 1)
                        if b:
                            tops_of(row, b - 1)
                    tops_of(row, NB - 1)
                    eng.wait_ge(read, row * SLOTS + 2 * SLOTS)
                    eng.tensor_reduce(top[:], tops[:].rearrange("p s h o -> p (h o) s"), AX_X, ALU.max).then_inc(row_done, 1)
                    eng.wait_ge(row_done, 2 * row + 1)
                    here = k.peak[:, bass.ds(row, 1), :].rearrange("p a b -> p (a b)")
                    eng.tensor_tensor(here, here, top[:], ALU.max).then_inc(row_done, 1)
                    eng.wait_ge(row_done, 2 * row + 2)

            @block.scalar
            def _(eng):
                with eng.Fori(0, CH) as row:
                    eng.wait_ge(scored, row * SLOTS + SLOTS)
                    for own, table in ((query, k.qt), (own_key, k.kt)):
                        eng.copy(flat(own[:]), table[:, bass.ds(row, 1), :, :].rearrange("p a b c -> p (a b c)"))\
                           .then_inc(query_ready, 1)
                    for b in range(NB):
                        eng.wait_ge(counted_, done(row, b))
                        eng.wait_ge(scored, row * SLOTS + (SLOTS + (b - 1) * BT))
                        eng.activation(flat(none[which[b]][:]), psA[which[b]][:], ACT.Relu, bias=1.0,
                                       scale=-1.0).then_inc(copied, 1)

            @block.tensor
            def _(eng):
                def score(row, b):
                    eng.wait_ge(copied, done(row, b))
                    if b == 0:
                        eng.wait_ge(query_ready, 2 * row + 2)
                    for n in range(BT):
                        first, odd = n // 2 * 2, n % 2
                        eng.wait_ge(read, row * SLOTS + (SLOTS + (b - 1) * BT + n + 1))
                        eng.matmul(psS[n][:].rearrange("p (s h t) -> p s h t", s=2, h=H // 2), k.neg_ident[:],
                                   none[which[b]][:, first:first + 2, :].unsqueeze(2)
                                   .to_broadcast([P, 2, H // 2, P]), start=True, stop=False)
                        rows = slice(64 * odd, 64 * odd + QS)
                        for m in range(4):
                            s, pair = b * BT + first + m // 2, m % 2
                            key = k.kt[rows, s, pair, :] if s < CH else own_key[rows, pair, :]
                            last = eng.matmul(psS[n][:, m * P:(m + 1) * P], query[rows, pair, :], key,
                                              start=False, stop=(m == 3))
                        last.then_inc(scored, 1)

                with eng.Fori(0, CH) as row:
                    for b in range(NB):
                        eng.wait_ge(hot_ready, row * (2 * NB) + (2 * b + 2))
                        eng.wait_ge(copied, done(row, b - 2))
                        for j in range(BT):
                            last = eng.matmul(psA[which[b]][:, j * P:(j + 1) * P], hot[which[b]][:, 0, j, :],
                                              hot[which[b]][:, 1, j, :], start=True, stop=True)
                        last.then_inc(counted_, 1)
                        if b:
                            score(row, b - 1)
                    score(row, NB - 1)


def gather_weights(eng, hot, psT, ident, signal):
    for j in range(BT):
        last = eng.transpose(psT[:, j * P:(j + 1) * P], hot[:, j, :], ident[:])
    last.then_inc(signal, 1)


LAG_SCATTER = 3
RING = 5


def ring(b):
    return RING - 1 if b == NB - 1 else b % (RING - 1)


def attend_phase(nc, k):
    with Phase(nc, "attend") as ph:
        hot_src = [ph.sb(f"hot_src{i}", [P, BT, P], F32) for i in range(RING)]
        hot_dst = [ph.sb(f"hot_dst{i}", [P, BT, P], BF16) for i in range(3)]
        sel_src = [ph.sb(f"sel_src{i}", [P, BT, P], BF16) for i in range(3)]
        sel_dst = [ph.sb(f"sel_dst{i}", [P, BT, P], BF16) for i in range(3)]
        query = [ph.sb(f"query{i}", [P, BT, H * DH + H], F32) for i in range(2)]
        prod = [ph.sb(f"prod{i}", [P, BT, H * DH], F32) for i in range(3)]
        logit = [ph.sb(f"logit{i}", [P, 2, BT, H], F32) for i in range(3)]
        msg = [ph.sb(f"msg{i}", [P, BT, D + H], F32) for i in range(RING)]
        psTs, psTd = ph.ps("psTs", [P, BT * P], F32), ph.ps("psTd", [P, BT * P], BF16)
        psQ = [ph.ps(f"psQ{i}", [P, 512], F32) for i in range(2)]
        psK = [ph.ps(f"psK{i}", [P, 512], F32) for i in range(2)]
        acc = ph.ps("acc", [P, 512], F32)
        hot_ready, turned, copied = ph.sem("hot_ready"), ph.sem("turned", NB), ph.sem("copied", NB)
        gathered, chain, weighed = ph.sem("gathered", NB), ph.sem("chain"), ph.sem("weighed", NB)
        msg_ready, scattered = ph.sem("msg_ready", NB), ph.sem("scattered", NB)
        row_read, logits, query_ready = ph.sem("row_read", 1), ph.sem("logits", NB), ph.sem("query_ready", NB)
        ph.begin()
        three = [2 if b == NB - 1 else b % 2 for b in range(NB)]
        QW, KW = H * DH + H, H * DH + D

        with nc.Block() as block:

            @block.vector
            def _(eng):
                def start(row, b):
                    eng.wait_ge(scattered, done(row, b - RING + 1))
                    eng.wait_ge(turned, done(row, b - 2))
                    for h, w in ((hot_src[ring(b)], SRC), (hot_dst[three[b]], DST)):
                        eng.tensor_tensor(h[:], bcast_mid(k.iota[:], BT),
                                          bcast_last(flat(k.by_src[:, w, bass.ds(row, 1), b * BT:(b + 1) * BT]), P),
                                          ALU.is_equal).then_inc(hot_ready, 1)

                def score(row, b):
                    q = query[b % 2]
                    kv = psK[b % 2][:, 0:BT * KW].rearrange("p (t c) -> p t c", c=KW)
                    eng.wait_ge(query_ready, done(row, b))
                    eng.wait_ge(weighed, done(row, b - 2))
                    eng.tensor_tensor(prod[three[b]][:], q[:, :, 0:H * DH], kv[:, :, 0:H * DH], ALU.mult)\
                       .then_inc(chain, 1)
                    eng.wait_ge(chain, row * (2 * NB) + (2 * b + 1))
                    eng.tensor_reduce(flat(logit[three[b]][:, 0, :, :]),
                                      flat(prod[three[b]][:]).rearrange("p (s d) -> p s d", d=DH),
                                      AX_X, ALU.add).then_inc(chain, 1)
                    eng.wait_ge(chain, row * (2 * NB) + (2 * b + 2))
                    eng.tensor_tensor(logit[three[b]][:, 1, :, :], logit[three[b]][:, 0, :, :], q[:, :, H * DH:],
                                      ALU.subtract).then_inc(logits, 1)

                def message(row, b):
                    kv = psK[b % 2][:, 0:BT * KW].rearrange("p (t c) -> p t c", c=KW)
                    m = msg[ring(b)]
                    eng.wait_ge(weighed, done(row, b))
                    for j in range(BT):
                        last = eng.tensor_tensor(m[:, j, 0:D].rearrange("p (h v) -> p h v", h=H),
                                                 kv[:, j, H * DH:].rearrange("p (h v) -> p h v", h=H),
                                                 bcast_last(m[:, j, D:], DV), ALU.mult)
                    last.then_inc(msg_ready, 1)

                with eng.Fori(0, CH) as row:
                    for b in range(NB + 2):
                        if b < NB:
                            start(row, b)
                        if 1 <= b <= NB:
                            score(row, b - 1)
                        if b >= 2:
                            message(row, b - 2)
                    eng.wait_ge(scattered, done(row, NB - 1))
                    here = flat(k.sums[:, bass.ds(row, 1), 0:D + H])
                    eng.tensor_tensor(here, here, acc[:, 0:D + H], ALU.add).then_inc(row_read, 1)

            @block.scalar
            def _(eng):
                def copy(row, b):
                    eng.wait_ge(turned, done(row, b))
                    eng.wait_ge(gathered, done(row, b - 2))
                    eng.copy(flat(sel_src[three[b]][:]), psTs[:])
                    eng.copy(flat(sel_dst[three[b]][:]), psTd[:]).then_inc(copied, 1)

                def weigh(row, b):
                    eng.wait_ge(logits, done(row, b))
                    eng.wait_ge(scattered, done(row, b - RING + 1))
                    eng.activation(msg[ring(b)][:, :, D:], logit[three[b]][:, 1, :, :], ACT.Exp)\
                       .then_inc(weighed, 1)

                def copy_query(row, b):
                    eng.wait_ge(gathered, done(row, b))
                    eng.wait_ge(logits, done(row, max(b - 2, -1)))
                    eng.copy(flat(query[b % 2][:]), psQ[b % 2][:, 0:BT * QW]).then_inc(query_ready, 1)

                with eng.Fori(0, CH) as row:
                    for b in range(NB + 2):
                        if b < NB:
                            copy(row, b)
                        if 1 <= b <= NB:
                            copy_query(row, b - 1)
                        if b >= 2:
                            weigh(row, b - 2)

            @block.tensor
            def _(eng):
                def turn(row, b):
                    eng.wait_ge(hot_ready, row * (2 * NB) + (2 * b + 2))
                    eng.wait_ge(copied, done(row, b - 1))
                    for j in range(BT):
                        eng.transpose(psTs[:, j * P:(j + 1) * P], hot_src[ring(b)][:, j, :], k.ident[:])
                    gather_weights(eng, hot_dst[three[b]], psTd, k.identb, turned)

                def gather(row, b):
                    eng.wait_ge(copied, done(row, b))
                    eng.wait_ge(msg_ready, done(row, max(b - 2, -1)))
                    for j in range(BT):
                        for part in range(3):
                            eng.matmul(psQ[b % 2][:, j * QW:(j + 1) * QW], sel_src[three[b]][:, j, :],
                                       flat(k.qm[:, bass.ds(row, 1), part, :]), start=(part == 0), stop=(part == 2))
                        for part in range(3):
                            last = eng.matmul(psK[b % 2][:, j * KW:(j + 1) * KW], sel_dst[three[b]][:, j, :],
                                              flat(k.kv[:, chunk_of(row, b, j), part, :]),
                                              start=(part == 0), stop=(part == 2))
                    last.then_inc(gathered, 1)

                def scatter(row, b):
                    eng.wait_ge(msg_ready, done(row, b))
                    if b == 0:
                        eng.wait_ge(row_read, row + 1)
                    for j in range(BT):
                        last = eng.matmul(acc[:, 0:D + H], hot_src[ring(b)][:, j, :], msg[ring(b)][:, j, :],
                                          start=(b == 0 and j == 0), stop=(b == NB - 1 and j == BT - 1))
                    last.then_inc(scattered, 1)

                with eng.Fori(0, CH) as row:
                    for b in range(NB + LAG_SCATTER):
                        if b < NB:
                            turn(row, b)
                        if 1 <= b <= NB:
                            gather(row, b - 1)
                        if b >= LAG_SCATTER:
                            scatter(row, b - LAG_SCATTER)


HALVES = ((0, 7 * BT), (7 * BT, SLOTS))


def message_phase(nc, k, rnd):
    with Phase(nc, "message") as ph:
        hot_dst = [ph.sb(f"hot_dst{i}", [P, BT, P], F32) for i in range(RING)]
        hot_src = [ph.sb(f"hot_src{i}", [P, BT, P], BF16) for i in range(3)]
        sel_src = [ph.sb(f"sel_src{i}", [P, BT, P], BF16) for i in range(3)]
        edge = [ph.sb(f"edge{i}", [P, b - a, D], F32) for i, (a, b) in enumerate(HALVES)]
        raw = [ph.sb(f"raw{i}", [P, BT, D], F32) for i in range(3)]
        msg = [ph.sb(f"msg{i}", [P, BT, D], F32) for i in range(RING)]
        psT = [ph.ps(f"psT{i}", [P, BT * P], BF16) for i in range(3)]
        psG = [ph.ps(f"psG{i}", [P, 512], F32) for i in range(3)]
        acc = ph.ps("acc", [P, 512], F32)
        hot_ready, turned, copied = ph.sem("hot_ready"), ph.sem("turned", NB), ph.sem("copied", NB)
        gathered, added, made = ph.sem("gathered", NB), ph.sem("added", NB), ph.sem("made", NB)
        scattered, row_read = ph.sem("scattered", NB), ph.sem("row_read", 1)
        here_in = [ph.sem(f"here_in{i}") for i in range(2)]
        ph.begin()
        three = [2 if b == NB - 1 else b % 2 for b in range(NB)]
        rows = k.edge_rows.rearrange("(p t) d -> p t d", p=P)
        with nc.Block() as block:

            @block.sync
            def _(eng):
                with eng.Fori(0, CH) as row:
                    for n, (a, b) in enumerate(HALVES):
                        with eng.If(rnd < 1):
                            eng.wait_ge(added, done(row, b // BT - 1 - NB))
                            eng.dma_start(edge[n][:], rows[:, bass.ds(row * SLOTS + a, b - a), :])\
                               .then_inc(here_in[n], 16)
                        with eng.Else():
                            eng.wait_ge(added, done(row, b // BT - 1 - NB))
                            eng.dma_start(edge[n][:], rows[:, bass.ds(MAIN - 1 + rnd, 1), :]
                                          .to_broadcast([P, b - a, D])).then_inc(here_in[n], 16)

            @block.vector
            def _(eng):
                def start(row, b):
                    eng.wait_ge(scattered, done(row, b - RING + 1))
                    eng.wait_ge(turned, done(row, b - 2))
                    for h, w in ((hot_src[three[b]], SRC), (hot_dst[ring(b)], DST)):
                        eng.tensor_tensor(h[:], bcast_mid(k.iota[:], BT),
                                          bcast_last(flat(k.by_dst[:, w, bass.ds(row, 1), b * BT:(b + 1) * BT]), P),
                                          ALU.is_equal).then_inc(hot_ready, 1)

                def add(row, b):
                    eng.wait_ge(gathered, done(row, b))
                    eng.wait_ge(made, done(row, b - 2))
                    half = int(b * BT >= HALVES[0][1])
                    first, last = (HALVES[half][n] for n in (0, 1))
                    if b * BT == first:
                        eng.wait_ge(here_in[half], row * 16 + 16)
                    s = b * BT - first
                    eng.tensor_tensor(flat(raw[three[b]][:]), psG[three[b]][:, 0:BT * D],
                                      flat(edge[half][:, s:s + BT, :]), ALU.add).then_inc(added, 1)

                with eng.Fori(0, CH) as row:
                    for b in range(NB + 1):
                        if b < NB:
                            start(row, b)
                        if b:
                            add(row, b - 1)
                    eng.wait_ge(scattered, done(row, NB - 1))
                    here = flat(k.sums[:, bass.ds(row, 1), 0:D])
                    eng.tensor_tensor(here, here, acc[:, 0:D], ALU.add).then_inc(row_read, 1)

            @block.scalar
            def _(eng):
                def copy(row, b):
                    eng.wait_ge(turned, done(row, b))
                    eng.wait_ge(gathered, done(row, b - 2))
                    eng.copy(flat(sel_src[three[b]][:]), psT[three[b]][:]).then_inc(copied, 1)

                def rectify(row, b):
                    eng.wait_ge(added, done(row, b))
                    eng.wait_ge(scattered, done(row, b - RING + 1))
                    eng.activation(flat(msg[ring(b)][:]), flat(raw[three[b]][:]), ACT.Relu).then_inc(made, 1)

                with eng.Fori(0, CH) as row:
                    for b in range(NB + 1):
                        if b < NB:
                            copy(row, b)
                        if b:
                            rectify(row, b - 1)

            @block.tensor
            def _(eng):
                def turn(row, b):
                    eng.wait_ge(hot_ready, row * (2 * NB) + (2 * b + 2))
                    eng.wait_ge(copied, done(row, b - 2))
                    gather_weights(eng, hot_src[three[b]], psT[three[b]], k.identb, turned)

                def gather(row, b):
                    eng.wait_ge(copied, done(row, b))
                    eng.wait_ge(added, done(row, b - 2))
                    for j in range(BT):
                        for part in range(3):
                            last = eng.matmul(psG[three[b]][:, j * D:(j + 1) * D], sel_src[three[b]][:, j, :],
                                              flat(k.table[:, chunk_of(row, b, j), part, :]),
                                              start=(part == 0), stop=(part == 2))
                    last.then_inc(gathered, 1)

                def scatter(row, b):
                    eng.wait_ge(made, done(row, b))
                    if b == 0:
                        eng.wait_ge(row_read, row + 1)
                    for j in range(BT):
                        last = eng.matmul(acc[:, 0:D], hot_dst[ring(b)][:, j, :], msg[ring(b)][:, j, :],
                                          start=(b == 0 and j == 0), stop=(b == NB - 1 and j == BT - 1))
                    last.then_inc(scattered, 1)

                with eng.Fori(0, CH) as row:
                    for b in range(NB + LAG_SCATTER):
                        if b < NB:
                            turn(row, b)
                        if 1 <= b <= NB:
                            gather(row, b - 1)
                        if b >= LAG_SCATTER:
                            scatter(row, b - LAG_SCATTER)


DENSE = 7
assert CH % DENSE == 0


def dense_phase(nc, k, name, rows, weight, width, result, bias=None):
    with Phase(nc, name) as ph:
        staged_rows = ph.sb("staged_rows", [P, DENSE, D], F32)
        turned_rows = ph.sb("turned_rows", [D, DENSE, P], F32)
        staged, turning = ph.sem("staged"), ph.sem("turning")
        psT = ph.ps("psT", [D, 8 * P], F32)
        psY = ph.ps("psY", [P, 8 * P], F32)
        turned, copied = ph.sem("turned"), ph.sem("copied")
        multiplied, written = ph.sem("multiplied", 1), ph.sem("written", 1)
        ph.begin()
        with nc.Block() as block:

            @block.tensor
            def _(eng):
                with eng.Fori(0, CH // DENSE) as g:
                    eng.wait_ge(staged, g + 1)
                    eng.sem_inc(turning, 1)
                    for c in range(DENSE):
                        last = eng.transpose(psT[:, c * P:(c + 1) * P], staged_rows[:, c, :], k.ident[:])
                    last.then_inc(turned, 1)
                    eng.wait_ge(copied, g + 1)
                    eng.wait_ge(written, g + 1)
                    for c in range(DENSE):
                        last = eng.matmul(psY[:, c * P:c * P + width], turned_rows[:, c, :], weight[:],
                                          start=True, stop=True)
                    last.then_inc(multiplied, 1)

            @block.scalar
            def _(eng):
                with eng.Fori(0, CH // DENSE) as g:
                    eng.wait_ge(multiplied, g + 1)
                    eng.copy(staged_rows[:], rows[:, bass.ds(g * DENSE, DENSE), :]).then_inc(staged, 1)
                    eng.wait_ge(turned, g + 1)
                    eng.copy(flat(turned_rows[:]), psT[:, 0:DENSE * P]).then_inc(copied, 1)

            @block.vector
            def _(eng):
                y = psY[:, 0:DENSE * P].rearrange("p (c w) -> p c w", w=P)[:, :, 0:width]
                with eng.Fori(0, CH // DENSE) as g:
                    eng.wait_ge(multiplied, g + 2)
                    out = result[:, bass.ds(g * DENSE, DENSE), 0:width]
                    if bias is None:
                        eng.tensor_copy(out, y).then_inc(written, 1)
                    else:
                        eng.tensor_tensor(out, y, bcast_mid(bias[:, 0:width], DENSE), ALU.add).then_inc(written, 1)
                eng.wait_ge(written, CH // DENSE + 1)


def node_phase(nc, k, name, work):
    with Phase(nc, name) as ph:
        step = ph.sem("step")
        with nc.Block() as block:

            @block.vector
            def _(eng):
                work(eng, counted(eng, step))


def root_phase(nc, k, name, *rows):
    with Phase(nc, name) as ph:
        root = ph.sb("root", [P, len(rows), CH], F32)
        square = ph.sb("square", [P, len(rows), CH], F32)
        rooted, step = ph.sem("rooted"), ph.sem("step")
        with nc.Block() as block:

            @block.scalar
            def _(eng):
                for n, (row, factor) in enumerate(rows):
                    eng.activation(root[:, n, :], row, ACT.Sqrt).then_inc(rooted, 1)

            @block.vector
            def _(eng):
                link = counted(eng, step)
                eng.wait_ge(rooted, len(rows))
                link(eng.reciprocal(root[:], root[:]))
                link(eng.tensor_tensor(square[:], root[:], root[:], ALU.mult))
                for n, (row, factor) in enumerate(rows):
                    link(eng.tensor_tensor(square[:, n, :], square[:, n, :], row, ALU.mult))
                link(eng.tensor_scalar(square[:], square[:], -0.5, 1.5, ALU.mult, ALU.add))
                for n, (row, factor) in enumerate(rows):
                    link(eng.scalar_tensor_tensor(row, root[:, n, :], factor, square[:, n, :], ALU.mult, ALU.mult))


def norm_stats(eng, link, k):
    mean, var = k.stat[:, 0, :], k.stat[:, 1, :]
    centred, square = k.wide[:, :, 0:D], k.wide[:, :, D:2 * D]
    link(eng.tensor_reduce(mean, k.X[:], AX_X, ALU.add))
    link(eng.tensor_single_scalar(mean, mean, 1.0 / D, ALU.mult))
    link(eng.tensor_tensor(centred, k.X[:], bcast_last(mean, D), ALU.subtract))
    link(eng.tensor_tensor(square, centred, centred, ALU.mult))
    link(eng.tensor_reduce(var, square, AX_X, ALU.add))
    link(eng.tensor_scalar(var, var, 1.0 / D, 1e-5, ALU.mult, ALU.add))


def norm_relu(eng, link, k):
    link(eng.tensor_tensor(k.hidden[:], k.wide[:, :, 0:D], bcast_last(k.stat[:, 1, :], D), ALU.mult))
    link(eng.tensor_single_scalar(k.hidden[:], k.hidden[:], 0.0, ALU.max))


def split(eng, link, value, parts, rest):
    left = value
    for n, copies in enumerate(parts):
        for c in copies:
            link(eng.tensor_copy(c, left))
        if n < 2:
            link(eng.tensor_tensor(rest, left, copies[0], ALU.subtract))
            left = rest


def split_table(eng, link, k, value, width):
    split(eng, link, value, [[k.table[:, :, n, 0:width]] for n in range(3)], k.rest[:, :, 0:width])



def stacked_phase(nc, k, name, value, places, turned):
    with Phase(nc, name) as ph:
        stack = ph.sb("stack", [P, CH, H, 64], BF16)
        staged_rows = ph.sb("staged_rows", [P, DENSE, H, 64], BF16)
        staged = ph.sem("staged")
        rest = ph.sb("rest", [P, CH, H * DH], F32)
        psT = ph.ps("psT", [P, DENSE * 2 * P], BF16)
        step, turned_, copied = ph.sem("step"), ph.sem("turned"), ph.sem("copied")
        with nc.Block() as block:

            @block.vector
            def _(eng):
                link = counted(eng, step)
                link(eng.memset(stack[:], 0.0))
                heads = value.rearrange("p c (h d) -> p c h d", h=H)
                left = rest[:].rearrange("p c (h d) -> p c h d", h=H)
                for h in range(H):
                    split(eng, link, heads[:, :, h, :],
                          [[stack[:, :, h, DH * i:DH * (i + 1)] for i in where] for where in places],
                          left[:, :, h, :])

            @block.tensor
            def _(eng):
                with eng.Fori(0, CH // DENSE) as g:
                    eng.wait_ge(staged, g + 1)
                    for c in range(DENSE):
                        for pair in range(H // 2):
                            at = (2 * c + pair) * P
                            last = eng.transpose(psT[:, at:at + P],
                                                 flat(staged_rows[:, c, 2 * pair:2 * pair + 2, :]), k.identb[:])
                    last.then_inc(turned_, 1)

            @block.scalar
            def _(eng):
                eng.wait_ge(step, STACK_STEPS)
                with eng.Fori(0, CH // DENSE) as g:
                    eng.copy(staged_rows[:], stack[:, bass.ds(g * DENSE, DENSE), :, :]).then_inc(staged, 1)
                    eng.wait_ge(turned_, g + 1)
                    eng.copy(turned[:, bass.ds(g * DENSE, DENSE), :, :].rearrange("p a b c -> p (a b c)"), psT[:])\
                       .then_inc(copied, 1)


STACK_STEPS = 1 + H * (PARTS + 2)


def store_phase(nc, k):
    with Phase(nc, "store") as ph:
        stored = ph.sem("stored")
        with nc.Block() as block:

            @block.sync
            def _(eng):
                eng.dma_start(k.out[0:(CH - 1) * P, :].rearrange("(c p) d -> p c d", p=P), k.X[:, 0:CH - 1, :])\
                   .then_inc(stored, 16)
                eng.dma_start(k.out[(CH - 1) * P:N_NODES, :], k.X[0:TAIL, CH - 1, :]).then_inc(stored, 16)
                eng.wait_ge(stored, 32)


def program(nc, dram, out):
    k = Kernel()
    k.x, k.src, k.dst, k.edge_attr = (dram[n] for n in ("x", "src", "dst", "edge_attr_64"))
    k.out = out
    k.edge_meta = nc.dram_tensor("edge_meta", (P * NT, 2), F32, kind="Internal").ap()
    k.edge_rows = nc.dram_tensor("edge_rows", (P * NT, D), F32, kind="Internal").ap()
    with ExitStack() as ctx:
        def sb(name, shape, dt):
            return ctx.enter_context(nc.sbuf_tensor(name, shape, dt))

        k.sent = [ctx.enter_context(nc.semaphore(f"sent{i}")) for i in range(2)]
        k.X = sb("X", [P, CH, D], F32)
        k.ident, k.identb = sb("ident", [P, P], F32), sb("identb", [P, P], BF16)
        k.neg_ident = sb("neg_ident", [P, P], BF16)
        k.later = sb("later", [P, EP], F32)
        k.iota = sb("iota", [P, P], BF16)
        k.slot_row = sb("slot_row", [P, 1], F32)
        k.deg = sb("deg", [P, 2, CH], F32)
        k.rounds = sb("rounds", [1, 1], I32)
        k.sums = sb("sums", [P, CH, D + H], F32)
        k.hidden = sb("hidden", [P, CH, D], F32)
        k.wide = sb("wide", [P, CH, 2 * D], F32)
        k.stat = sb("stat", [P, 6, CH], F32)
        weight = {n: sb(n, list(dram[n].shape), F32) for n in dram if "_W" in n}
        bias = {n: sb(n, [P, dram[n].shape[0]], F32) for n in dram if "_b" in n}
        k.weights = [(weight[n][:], dram[n]) for n in weight]
        k.weights += [(bias[n][:], dram[n].rearrange("(a n) -> a n", a=1).to_broadcast([P, dram[n].shape[0]]))
                      for n in bias]
        setup_phase(nc, k)
        place_phase(nc, k)
        k.n_rounds = nc.values_load(k.rounds[0:1, 0:1], min_val=1, max_val=ET + 1)
        k.by_dst = sb("by_dst", [P, 2, CH, SLOTS], F32)
        k.by_src = sb("by_src", [P, 2, CH, SLOTS], F32)
        tiles_phase(nc, k, None)
        sums, hidden, wide = k.sums, k.hidden, k.wide
        rows_of = sums[:, :, 0:D]
        dinv = k.stat[:, 3, :]
        tables = ExitStack()

        def table(width):
            k.table = tables.enter_context(nc.sbuf_tensor(f"table{nc.next_id()}", [P, CH, 3, width], BF16))
            k.rest = tables.enter_context(nc.sbuf_tensor(f"rest{nc.next_id()}", [P, CH, width], F32))

        table(D + 1)

        def first(eng, link):
            link(eng.tensor_single_scalar(dinv, k.deg[:, DST, :], 1.0, ALU.add))
            norm_stats(eng, link, k)

        def scaled(eng, link):
            link(eng.tensor_tensor(wide[:, :, 0:D], wide[:, :, 0:D], bcast_last(dinv, D), ALU.mult))
            split_table(eng, link, k, wide[:, :, 0:D], D)
            link(eng.memset(sums[:], 0.0))

        def convolved(b):
            def work(eng, link):
                link(eng.tensor_tensor(rows_of, rows_of, wide[:, :, 0:D], ALU.add))
                link(eng.tensor_tensor(rows_of, rows_of, bcast_last(dinv, D), ALU.mult))
                link(eng.tensor_tensor(rows_of, rows_of, bcast_mid(b[:], CH), ALU.add))
                link(eng.tensor_single_scalar(hidden[:], rows_of, 0.0, ALU.max))
            return work

        var = k.stat[:, 1, :]
        node_phase(nc, k, "stats0", first)
        root_phase(nc, k, "root0", (dinv, 1.0), (var, 1.0))
        node_phase(nc, k, "norm0", lambda eng, link: norm_relu(eng, link, k))
        for n in (1, 2):
            dense_phase(nc, k, f"conv{n}_dense", hidden, weight[f"L0_gnn_W{n}"], D, wide)
            node_phase(nc, k, f"conv{n}_table", scaled)
            in_rounds(nc, k, lambda rnd: sum_phase(nc, k, f"conv{n}", SRC, DST, k.by_dst, k.table, D))
            node_phase(nc, k, f"conv{n}_end", convolved(bias[f"L0_gnn_b{n}"]))

        have = k.stat[:, 4, :]

        def layer1_stats(eng, link):
            link(eng.tensor_tensor(k.X[:], k.X[:], hidden[:], ALU.add))
            norm_stats(eng, link, k)
            link(eng.tensor_single_scalar(have, k.deg[:, DST, :], 1.0, ALU.max))

        def layer1(eng, link):
            norm_relu(eng, link, k)
            link(eng.tensor_single_scalar(dinv, k.deg[:, DST, :], 0.0, ALU.is_gt))
            link(eng.tensor_tensor(dinv, dinv, have, ALU.mult))
            link(eng.tensor_tensor(wide[:, :, 0:D], hidden[:], bcast_last(dinv, D), ALU.mult))
            link(eng.tensor_copy(wide[:, :, D], dinv))
            split_table(eng, link, k, wide[:, :, 0:D + 1], D + 1)
            link(eng.memset(sums[:], 0.0))

        def layer1_sums(eng, link):
            link(eng.tensor_tensor(sums[:, :, 0:D + 1], sums[:, :, 0:D + 1], bcast_last(dinv, D + 1), ALU.mult))
            link(eng.tensor_tensor(hidden[:], hidden[:], rows_of, ALU.mult))
            link(eng.tensor_tensor(bias["L1_gnn_b1"][:], bias["L1_gnn_b1"][:], bias["L1_gnn_b2"][:], ALU.add))

        def layer1_end(eng, link):
            link(eng.tensor_tensor(rows_of, wide[:, :, 0:D], wide[:, :, D:], ALU.add))
            link(eng.tensor_tensor(hidden[:], bcast_last(sums[:, :, D], D), bcast_mid(bias["L1_gnn_b1"][:], CH),
                                   ALU.mult))
            link(eng.tensor_tensor(rows_of, rows_of, hidden[:], ALU.add))
            link(eng.scalar_tensor_tensor(hidden[:], rows_of, 0.2, rows_of, ALU.mult, ALU.max))
            link(eng.tensor_tensor(k.X[:], k.X[:], hidden[:], ALU.add))

        node_phase(nc, k, "layer1_stats", layer1_stats)
        root_phase(nc, k, "root1", (have, 1.0), (var, 1.0))
        node_phase(nc, k, "layer1_table", layer1)
        in_rounds(nc, k, lambda rnd: sum_phase(nc, k, "layer1", DST, SRC, k.by_src, k.table, D + 1))
        tables.close()
        node_phase(nc, k, "layer1_sums", layer1_sums)
        dense_phase(nc, k, "layer1_dense1", rows_of, weight["L1_gnn_W1"], D, wide)
        dense_phase(nc, k, "layer1_dense2", hidden, weight["L1_gnn_W2"], D, wide[:, :, D:])
        node_phase(nc, k, "layer1_end", layer1_end)

        def layer2_stats(eng, link):
            norm_stats(eng, link, k)
            link(eng.tensor_single_scalar(have, k.deg[:, SRC, :], 1.0, ALU.max))

        def queries(eng, link):
            link(eng.tensor_tensor(wide[:, :, 0:H * DH], wide[:, :, 0:H * DH], bcast_last(have, H * DH), ALU.mult))
            link(eng.memset(k.peak[:], -BIG))

        node_phase(nc, k, "layer2_stats", layer2_stats)
        root_phase(nc, k, "root2", (have, QK_SCALE), (var, 1.0))
        node_phase(nc, k, "norm2", lambda eng, link: norm_relu(eng, link, k))
        dense_phase(nc, k, "qkv", hidden, weight["L2_gnn_W_qkv"], 2 * D, wide, bias["L2_gnn_b_qkv"])
        k.peak = sb("peak", [P, CH, H], F32)
        node_phase(nc, k, "queries", queries)
        with nc.sbuf_tensor("qt", [P, CH, H // 2, P], BF16) as k.qt, \
                nc.sbuf_tensor("kt", [P, CH, H // 2, P], BF16) as k.kt:
            stacked_phase(nc, k, "stack_q", wide[:, :, 0:H * DH], ((0, 1, 4), (2, 3), (5,)), k.qt)
            stacked_phase(nc, k, "stack_k", wide[:, :, H * DH:2 * H * DH], ((0, 2, 5), (1, 3), (4,)), k.kt)
            in_rounds(nc, k, lambda rnd: max_phase(nc, k))
        with nc.sbuf_tensor("qm", [P, CH, 3, H * DH + H], BF16) as k.qm, \
                nc.sbuf_tensor("kv", [P, CH, 3, H * DH + D], BF16) as k.kv:
            with nc.sbuf_tensor("rest2", [P, CH, H * DH + D], F32) as rest:
                def attention_tables(eng, link):
                    q, kv = wide[:, :, 0:H * DH], wide[:, :, H * DH:]
                    split(eng, link, q, [[k.qm[:, :, n, 0:H * DH]] for n in range(3)], rest[:, :, 0:H * DH])
                    split(eng, link, k.peak[:], [[k.qm[:, :, n, H * DH:]] for n in range(3)], rest[:, :, 0:H])
                    split(eng, link, kv, [[k.kv[:, :, n, :]] for n in range(3)], rest[:])
                    link(eng.memset(sums[:], 0.0))

                node_phase(nc, k, "attention_tables", attention_tables)
            in_rounds(nc, k, lambda rnd: attend_phase(nc, k))

        def layer3(eng, link):
            link(eng.tensor_single_scalar(sums[:, :, D:], sums[:, :, D:], 1e-16, ALU.add))
            link(eng.reciprocal(sums[:, :, D:], sums[:, :, D:]))
            for h in range(H):
                link(eng.tensor_tensor(hidden[:, :, h * DV:(h + 1) * DV], sums[:, :, h * DV:(h + 1) * DV],
                                       bcast_last(sums[:, :, D + h], DV), ALU.mult))
            link(eng.tensor_tensor(k.X[:], k.X[:], hidden[:], ALU.add))
            norm_stats(eng, link, k)

        def layer3_table(eng, link):
            norm_relu(eng, link, k)
            split_table(eng, link, k, hidden[:], D)
            link(eng.memset(sums[:], 0.0))

        table(D)
        node_phase(nc, k, "layer3_stats", layer3)
        root_phase(nc, k, "root3", (var, 1.0))
        node_phase(nc, k, "layer3_table", layer3_table)
        in_rounds(nc, k, lambda rnd: message_phase(nc, k, rnd))
        tables.close()
        node_phase(nc, k, "layer3_sum", lambda eng, link:
                   link(eng.tensor_tensor(hidden[:], hidden[:], rows_of, ALU.add)))
        for n in (1, 2, 3):
            dense_phase(nc, k, f"layer3_dense{n}", hidden, weight[f"L3_gnn_W{n}"], D, wide, bias[f"L3_gnn_b{n}"])
            if n < 3:
                node_phase(nc, k, f"layer3_relu{n}", lambda eng, link:
                           link(eng.tensor_single_scalar(hidden[:], wide[:, :, 0:D], 0.0, ALU.max)))
        node_phase(nc, k, "layer3_end", lambda eng, link:
                   link(eng.tensor_tensor(k.X[:], k.X[:], wide[:, :, 0:D], ALU.add)))
        store_phase(nc, k)


def kernel(**inputs):
    import numpy as np
    import concourse.bacc as bacc
    from concourse.bass_utils import run_bass_kernel_spmd as run

    nc = bacc.Bacc("TRN2", target_bir_lowering=False, num_devices=1)
    laid = {n: np.ascontiguousarray(a.T if n[:2] in ("L1", "L3") and a.ndim == 2 else a)
            for n, a in ((n, np.asarray(a)) for n, a in inputs.items())}
    dram = {n: nc.dram_tensor(f"in_{n}", a.shape, mybir.dt.from_np(a.dtype), kind="ExternalInput").ap()
            for n, a in laid.items()}
    out = nc.dram_tensor("out", (N_NODES, D), F32, kind="ExternalOutput").ap()
    program(nc, dram, out)
    r = run(nc, [{f"in_{n}": a for n, a in laid.items()}], core_ids=[0])
    return r.results[0]["out"]
```

```python
import concourse.bass as bass
from concourse import mybir
from contextlib import ExitStack

F32 = mybir.dt.float32
BF16 = mybir.dt.bfloat16
I32 = mybir.dt.int32
ALU = mybir.AluOpType
ACT = mybir.ActivationFunctionType
AX_X = mybir.AxisListType.X

P = 128
N_NODES, D = 6250, 64
N_EDGES = 206250
CH = -(-N_NODES // P)
TAIL = N_NODES - (CH - 1) * P
EP = 125
ET = N_EDGES // EP
GROUP = 5
DIAG = 4
SLOTS = CH + DIAG - 1
MAIN = CH * SLOTS
NT = MAIN + ET + 1
BT = 4
NB = SLOTS // BT
H, DH, DV = 4, 8, 16
QK_SCALE = float(D // H) ** -0.5
BIG = 1.0e30
PARTS = 6
QS = PARTS * DH
assert EP * ET == N_EDGES and NB * BT == SLOTS and ET % (2 * GROUP) == 0

SRC, DST = 0, 1


class Kernel:
    pass


def counted(eng, sem):
    n = [0]

    def link(ins):
        n[0] += 1
        ins.then_inc(sem, 1)
        eng.wait_ge(sem, n[0])

    return link


def end_phase(nc, sems):
    for s in sems:
        nc.gpsimd.sem_clear(s)
    nc.all_engine_barrier()


class Phase:

    def __init__(self, nc, name):
        self.nc, self.name, self.sems, self.starts, self.ctx = nc, f"p{nc.next_id()}_{name}", [], [], ExitStack()

    def __enter__(self):
        self.ctx.__enter__()
        return self

    def sem(self, name, start=0):
        s = self.ctx.enter_context(self.nc.semaphore(f"{self.name}_{name}"))
        self.sems.append(s)
        if start:
            self.starts.append((s, start))
        return s

    def begin(self):
        for s, start in self.starts:
            self.nc.gpsimd.sem_inc(s, start)
        self.nc.all_engine_barrier()

    def sb(self, name, shape, dt):
        return self.ctx.enter_context(self.nc.sbuf_tensor(f"{self.name}_{name}", shape, dt))

    def ps(self, name, shape, dt):
        return self.ctx.enter_context(self.nc.psum_tensor(f"{self.name}_{name}", shape, dt))

    def __exit__(self, *a):
        if a[0] is None:
            end_phase(self.nc, self.sems)
        return self.ctx.__exit__(*a)


def bcast_mid(ap, n):
    return ap.unsqueeze(1).to_broadcast([ap.shape[0], n, ap.shape[1]])


def bcast_last(ap, n):
    return ap.unsqueeze(2).to_broadcast([ap.shape[0], ap.shape[1], n])


def setup_phase(nc, k):
    with Phase(nc, "setup") as ph:
        made, loaded, filled = ph.sem("made"), ph.sem("loaded"), ph.sem("filled")
        conv = ph.sem("converted")
        idn = ph.sem("identity")
        blank = ph.sb("blank", [P, 2 * NT], F32)
        ioti = ph.sb("ioti", [P, P], I32)
        slot_row = ph.sb("slot_row", [P, 1], I32)
        with nc.Block() as block:

            @block.gpsimd
            def _(eng):
                eng.iota(ioti[:], pattern=[[1, P]], base=0, channel_multiplier=0).then_inc(made, 1)
                eng.iota(slot_row[:], pattern=[[0, 1]], base=MAIN, channel_multiplier=NT).then_inc(made, 1)
                eng.memset(k.ident[:], 0.0).then_inc(idn, 1)
                eng.memset(k.identb[:], 0.0).then_inc(idn, 1)
                eng.memset(k.later[:], 1.0).then_inc(idn, 1)
                eng.memset(k.neg_ident[:], 0.0).then_inc(idn, 1)
                eng.wait_ge(idn, 4)
                for m, fill in ((k.ident, 1.0), (k.identb, 1.0), (k.neg_ident, -BIG)):
                    eng.affine_select(out=m[:], in_=m[:], compare_op=ALU.not_equal, fill=fill, base=0,
                                      pattern=[[-1, P]], channel_multiplier=1).then_inc(idn, 1)
                eng.affine_select(out=k.later[:], in_=k.later[:], compare_op=ALU.is_gt, fill=0.0, base=0,
                                  pattern=[[-1, EP]], channel_multiplier=1).then_inc(idn, 1)
                eng.wait_ge(idn, 8)
                eng.wait_ge(conv, 1)
                for b in range(2):
                    half = slice(b * P // 2, (b + 1) * P // 2)
                    eng.dma_start(k.edge_meta.rearrange("(p t) c -> p (t c)", p=P)[half, :], blank[half, :])\
                       .then_inc(k.sent[b], 16)
                for b in range(2):
                    eng.wait_ge(k.sent[b], 16)

            @block.vector
            def _(eng):
                eng.memset(blank[:], -1.0e6).then_inc(conv, 1)
                eng.memset(k.X[:], 0.0).then_inc(conv, 1)
                eng.wait_ge(made, 2)
                eng.tensor_copy(k.iota[:], ioti[:]).then_inc(conv, 1)
                eng.tensor_copy(k.slot_row[:], slot_row[:]).then_inc(conv, 1)
                eng.wait_ge(conv, 4)

            @block.sync
            def _(eng):
                eng.wait_ge(conv, 2)
                for a, b in ((0, CH // 2), (CH // 2, CH - 1)):
                    eng.dma_start(k.X[:, a:b, :], k.x[a * P:b * P, :].rearrange("(c p) d -> p c d", p=P))\
                       .then_inc(loaded, 16)
                eng.dma_start(k.X[0:TAIL, CH - 1, :], k.x[(CH - 1) * P:N_NODES, :]).then_inc(loaded, 16)
                for dst, w in k.weights:
                    eng.dma_start(dst, w).then_inc(loaded, 16)
                attr = k.edge_rows.rearrange("(p t) c -> p (t c)", p=P)
                for c in range(D // 2):
                    eng.dma_start(attr[:, c * 2 * NT:(c + 1) * 2 * NT], blank[:]).then_inc(filled, 16)
                eng.wait_ge(filled, 16 * (D // 2))
                eng.wait_ge(loaded, 16 * (3 + len(k.weights)))


def place_phase(nc, k):
    with Phase(nc, "place") as ph:
        ends = ph.sb("ends", [EP, 2, ET], I32)
        local = ph.sb("local", [EP, 2, ET + GROUP], F32)
        chunk = ph.sb("chunk", [EP, 2, ET + GROUP], F32)
        whole = ph.sb("whole", [EP, 2, ET], F32)
        tmpi = ph.sb("tmpi", [EP, 2, ET], I32)
        hot_c = [ph.sb(f"hot_chunk{i}", [EP, GROUP, 2, CH], BF16) for i in range(2)]
        hot_l = [ph.sb(f"hot_local{i}", [EP, GROUP, 2, P], BF16) for i in range(2)]
        hot_t = [ph.sb(f"hot_t{i}", [2 * CH, GROUP, EP], BF16) for i in range(2)]
        cum_hi, cum_lo = ph.sb("cum_hi", [CH, CH], BF16), ph.sb("cum_lo", [CH, CH], BF16)
        zero = ph.sb("zero", [EP, P], BF16)
        junk = ph.sb("junk", [EP, GROUP, P], F32)
        junk2 = ph.sb("junk2", [EP, GROUP, CH], F32)
        rin, rbe = ph.sb("rank_in_tile", [EP, GROUP], F32), ph.sb("rank_before", [EP, GROUP], F32)
        t = ph.sb("t", [EP, 12, GROUP], F32)
        scan = ph.sb("scan", [EP, 4, 4 + GROUP], F32)
        spilled = ph.sb("spilled", [EP, 1], F32)
        spill_row = ph.sb("spill_row", [1, 2], F32)
        index = [ph.sb(f"index{i}", [EP, GROUP], I32) for i in range(2)]
        meta = [ph.sb(f"meta{i}", [EP, GROUP, 2], F32) for i in range(2)]
        rows = [ph.sb(f"rows{i}", [EP, GROUP, D], F32) for i in range(2)]
        psT = [ph.ps(f"psT{i}", [2 * CH, GROUP, P], BF16) for i in range(2)]
        psS = ph.ps("same", [EP, 2 * 4, P], F32)
        psG = ph.ps("before", [EP, 512], F32)
        psC = ph.ps("counts", [CH, 512], F32)
        psD = ph.ps("degrees", [P, 512], F32)
        loaded, done = ph.sem("loaded"), ph.sem("converted")
        hot_ready, t_ready, t_copied = ph.sem("hot_ready"), ph.sem("t_ready"), ph.sem("t_copied")
        same_ready, count_ready, cum_ready = ph.sem("same_ready"), ph.sem("count_ready"), ph.sem("cum_ready", 1)
        ranked, idx_ready = ph.sem("ranked", 1), ph.sem("idx_ready")
        rows_in = [ph.sem(f"rows_in{i}") for i in range(2)]
        sent = k.sent
        chain = ph.sem("chain")
        fin, sending = ph.sem("fin"), ph.sem("sending")
        groups = ET // GROUP
        ph.begin()
        edge_rows = k.edge_attr.rearrange("(p t) d -> p t d", p=EP)
        with nc.Block() as block:

            @block.sync
            def _(eng):
                for w, a in ((SRC, k.src), (DST, k.dst)):
                    eng.dma_start(ends[:, w, :], a.rearrange("(p t) -> p t", p=EP)).then_inc(loaded, 16)
                with eng.Fori(0, groups // 2) as i:
                    for b in range(2):
                        eng.wait_ge(sent[b], i * (GROUP * 32) + 16)
                        eng.dma_start(rows[b][:], edge_rows[:, bass.ds((2 * i + b) * GROUP, GROUP), :])\
                           .then_inc(rows_in[b], 16)

            @block.gpsimd
            def _(eng):
                last_row = eng.alloc_register("last_row")
                eng.reg_mov(last_row, P * NT - 1)
                with eng.Fori(0, groups // 2) as i:
                    for b in range(2):
                        placed, brought = eng.snap(2 * i + b + 1), eng.snap(16 * i + 16)
                        eng.wait_ge(idx_ready, placed)
                        eng.wait_ge(rows_in[b], brought)
                        eng.sem_inc(sending, 1)
                        for j in range(GROUP):
                            at = bass.IndirectOffsetOnAxis(index[b][:, j:j + 1], 0)
                            eng.indirect_dma_start(k.edge_meta, at, meta[b][:, j, :], None,
                                                   bounds_check=last_row, oob_is_err=False).then_inc(sent[b], 16)
                            eng.indirect_dma_start(k.edge_rows, at, rows[b][:, j, :], None,
                                                   bounds_check=last_row, oob_is_err=False).then_inc(sent[b], 16)
                for b in range(2):
                    eng.wait_ge(sent[b], 16 + 32 * GROUP * (groups // 2))

            @block.vector
            def _(eng):
                link = counted(eng, done)
                eng.memset(zero[:], 0.0)
                eng.memset(spilled[:], 0.0)
                eng.memset(cum_hi[:], 0.0)
                eng.memset(cum_lo[:], 0.0)
                eng.memset(local[:, :, ET:], 0.0)
                eng.memset(chunk[:, :, ET:], 0.0)
                link(eng.memset(scan[:], 0.0))
                eng.wait_ge(loaded, 32)
                link(eng.tensor_single_scalar(tmpi[:], ends[:], 7, ALU.arith_shift_right))
                link(eng.tensor_copy(chunk[:, :, 0:ET], tmpi[:]))
                link(eng.tensor_copy(whole[:], ends[:]))
                link(eng.scalar_tensor_tensor(local[:, :, 0:ET], chunk[:, :, 0:ET], -float(P), whole[:], ALU.mult,
                                              ALU.add))

                def clink(n, ins):
                    ins.then_inc(chain, 1)
                    eng.wait_ge(chain, n)

                def one_hot(g, b, n):
                    hot, of, width = ((hot_c[b], chunk, CH), (hot_l[b], local, P))[n // 2]
                    eng.tensor_tensor(hot[:, :, n % 2, :], bcast_mid(k.iota[0:EP, 0:width], GROUP),
                                      bcast_last(of[:, n % 2, bass.ds(g * GROUP, GROUP)], width), ALU.is_equal)\
                       .then_inc(hot_ready, 1)

                for n in range(4):
                    one_hot(0, 0, n)
                with eng.Fori(0, groups // 2) as i:
                    for b in range(2):
                        g = 2 * i + b
                        steps = [0]

                        def step(ins, g=g, steps=steps):
                            steps[0] += 1
                            clink(g * CHAIN + steps[0], ins)

                        at = bass.ds(g * GROUP, GROUP)
                        step(eng.tensor_tensor(t[:, 0, :], chunk[:, SRC, at], chunk[:, DST, at], ALU.is_equal))
                        for j in range(GROUP):
                            eng.wait_ge(count_ready, g * GROUP + j + 1)
                            step(eng.tensor_scalar(cum_hi[:], psC[:, 0:CH], 32000.0, None, ALU.min))
                            eng.scalar_tensor_tensor(cum_lo[:], psC[:, 0:CH], 32000.0, cum_hi[:], ALU.min,
                                                     ALU.subtract).then_inc(cum_ready, 1)
                            if j == 0:
                                eng.wait_ge(same_ready, g + 1)
                            eng.scalar_tensor_tensor(junk[:, j, 0:EP], psS[:, j, 0:EP], 1.5, k.later[0:EP, :],
                                                     ALU.is_gt, ALU.mult, accum_out=rin[:, j:j + 1])
                            if j < 4:
                                one_hot(g + 1, 1 - b, j)
                        step(eng.tensor_tensor(junk2[:], psG[:, 0:GROUP * CH].rearrange("p (t c) -> p t c", c=CH),
                                               hot_c[b][:, :, DST, :], ALU.mult))
                        eng.tensor_reduce(rbe[:], junk2[:], AX_X, ALU.add).then_inc(ranked, 1)
                        eng.wait_ge(ranked, g + 2)
                        r, m1, m, q, e = (t[:, n, :] for n in (1, 2, 5, 4, 0))
                        no_slot, tile = scan[:, 0, 4:], t[:, 9, :]
                        base = steps[0]

                        def go(ins, steps=steps):
                            steps[0] += 1
                            ins.then_inc(chain, 1)

                        def after(n, g=g, base=base):
                            eng.wait_ge(chain, g * CHAIN + (base + n))

                        go(eng.tensor_tensor(r, rin[:], rbe[:], ALU.add))
                        eng.wait_ge(sent[b], i * (GROUP * 32) + 16)
                        go(eng.tensor_copy(meta[b][:].rearrange("p t w -> p w t"), whole[:, :, at]))
                        after(1)
                        go(eng.tensor_single_scalar(m1, r, 128.0, ALU.is_ge))
                        go(eng.scalar_tensor_tensor(t[:, 8, :], chunk[:, DST, at], float(SLOTS), chunk[:, SRC, at],
                                                    ALU.mult, ALU.add))
                        after(3)
                        go(eng.tensor_tensor(t[:, 6, :], m1, e, ALU.is_gt))
                        go(eng.scalar_tensor_tensor(t[:, 3, :], r, 256.0, m1, ALU.is_ge, ALU.add))
                        after(5)
                        go(eng.scalar_tensor_tensor(no_slot, r, 128.0 * DIAG, t[:, 6, :], ALU.is_ge, ALU.max))
                        after(6)
                        go(eng.scalar_tensor_tensor(m, r, 384.0, t[:, 3, :], ALU.is_ge, ALU.add))
                        after(7)
                        go(eng.tensor_tensor(scan[:, 1, 4:], no_slot, scan[:, 0, 3:3 + GROUP], ALU.add))
                        after(8)
                        go(eng.scalar_tensor_tensor(tile, m, float(CH - 1), chunk[:, SRC, at], ALU.add,
                                                    ALU.subtract))
                        after(9)
                        go(eng.tensor_tensor(scan[:, 2, 4:], scan[:, 1, 4:], scan[:, 1, 2:2 + GROUP], ALU.add))
                        after(10)
                        go(eng.tensor_tensor(t[:, 10, :], tile, m1, ALU.mult))
                        after(11)
                        go(eng.tensor_tensor(scan[:, 3, 4:], scan[:, 2, 4:], scan[:, 2, 0:GROUP], ALU.add))
                        after(12)
                        go(eng.tensor_tensor(t[:, 11, :], t[:, 10, :], t[:, 8, :], ALU.add))
                        after(13)
                        go(eng.tensor_scalar(t[:, 7, :], scan[:, 3, 4:], spilled[:], k.slot_row[0:EP, :],
                                             ALU.add, ALU.add))
                        go(eng.scalar_tensor_tensor(q, m, -128.0, r, ALU.mult, ALU.add))
                        after(15)
                        go(eng.tensor_tensor(t[:, 6, :], t[:, 7, :], no_slot, ALU.subtract))
                        after(16)
                        go(eng.scalar_tensor_tensor(t[:, 3, :], q, float(NT), t[:, 11, :], ALU.mult, ALU.add))
                        go(eng.tensor_tensor(spilled[:], spilled[:], scan[:, 3, 3 + GROUP:4 + GROUP], ALU.add))
                        after(18)
                        go(eng.tensor_tensor(t[:, 7, :], t[:, 6, :], t[:, 3, :], ALU.subtract))
                        after(20)
                        go(eng.tensor_tensor(t[:, 10, :], t[:, 7, :], no_slot, ALU.mult))
                        after(21)
                        eng.tensor_tensor(index[b][:], t[:, 10, :], t[:, 3, :], ALU.add).then_inc(idx_ready, 1)
                        assert steps[0] == CHAIN
                eng.wait_ge(fin, 2)
                eng.tensor_copy(k.deg[:, SRC, :], psD[:, 0:CH])
                eng.tensor_copy(k.deg[:, DST, :], psD[:, CH:2 * CH])
                eng.tensor_reduce(spill_row[0:1, 0:1], psC[0:1, 0:EP], AX_X, ALU.max).then_inc(fin, 1)
                eng.wait_ge(fin, 3)
                eng.tensor_scalar(k.rounds[:], spill_row[0:1, 0:1], 1.0, None, ALU.add).then_inc(fin, 1)
                eng.wait_ge(fin, 4)

            @block.scalar
            def _(eng):
                with eng.Fori(0, groups // 2) as i:
                    for b in range(2):
                        g = 2 * i + b
                        eng.wait_ge(t_ready, g + 1)
                        eng.copy(hot_t[b][:], psT[b][:, :, 0:EP])\
                           .then_inc(t_copied, 1)

            @block.tensor
            def _(eng):
                eng.wait_ge(done, 1)
                eng.matmul(psC[:, 0:CH], zero[:, 0:CH], zero[:, 0:CH], start=True, stop=True)
                eng.matmul(psD[:, 0:2 * CH], zero[:, :], zero[:, 0:2 * CH], start=True, stop=True)

                def turn(g, b):
                    eng.wait_ge(hot_ready, 4 * g + 4)
                    for j in range(GROUP):
                        last = eng.transpose(psT[b][:, j, 0:EP], hot_c[b][:, j, :, :].rearrange("p w c -> p (w c)"),
                                             k.identb[0:EP, 0:EP])
                    last.then_inc(t_ready, 1)

                turn(0, 0)
                with eng.Fori(0, groups // 2) as i:
                    for b in range(2):
                        g = 2 * i + b
                        eng.wait_ge(t_copied, g + 1)
                        eng.wait_ge(ranked, g + 1)
                        for j in range(GROUP):
                            last = eng.matmul(psS[:, j, 0:EP], hot_t[b][:, j, :], hot_t[b][:, j, :],
                                              start=True, stop=True)
                        last.then_inc(same_ready, 1)
                        for j in range(GROUP):
                            eng.wait_ge(cum_ready, g * GROUP + (j + 1))
                            before = psG[:, j * CH:(j + 1) * CH]
                            eng.matmul(before, hot_t[b][0:CH, j, :], cum_hi[:], start=True, stop=False)
                            eng.matmul(before, hot_t[b][0:CH, j, :], cum_lo[:], start=False, stop=True)
                            eng.matmul(psC[:, 0:CH], hot_c[b][:, j, SRC, :], hot_c[b][:, j, DST, :],
                                       start=False, stop=True, skip_group_check=True).then_inc(count_ready, 1)
                        turn(g + 1, 1 - b)
                        for j in range(GROUP):
                            for w in (SRC, DST):
                                eng.matmul(psD[:, w * CH:(w + 1) * CH], hot_l[b][:, j, w, :], hot_c[b][:, j, w, :],
                                           start=False, stop=True, skip_group_check=True)
                eng.wait_ge(chain, groups * CHAIN)
                eng.wait_ge(cum_ready, groups * GROUP + 1)
                eng.matmul(psC[0:1, 0:EP], spilled[:], k.ident[0:EP, 0:EP], start=True, stop=True).then_inc(fin, 2)


CHAIN = 1 + GROUP + 22


def tiles_phase(nc, k, tile):
    with Phase(nc, "tiles" if tile is None else "spill_tiles") as ph:
        raw = ph.sb("raw", [P, CH, SLOTS, 2] if tile is None else [P, 1, 1, 2], F32)
        loaded, made = ph.sem("loaded"), ph.sem("made")
        ph.begin()
        meta = k.edge_meta.rearrange("(p t) c -> p t c", p=P)
        with nc.Block() as block:

            @block.sync
            def _(eng):
                if tile is None:
                    eng.dma_start(raw[:], meta[:, 0:MAIN, :].rearrange("p (j s) c -> p j s c", s=SLOTS))\
                       .then_inc(loaded, 16)
                else:
                    eng.dma_start(raw[:, 0, :, :], meta[:, bass.ds(tile, 1), :]).then_inc(loaded, 16)
                eng.wait_ge(loaded, 16)

            @block.vector
            def _(eng):
                link = counted(eng, made)

                def ends(w, a, b):
                    if tile is None:
                        return raw[:, :, a:b, w]
                    return raw[:, :, :, w].to_broadcast([P, CH, b - a])

                chunks = k.iota[:, 0:CH]
                eng.wait_ge(loaded, 16)
                link(eng.scalar_tensor_tensor(k.by_dst[:, SRC, :, 0:CH], bcast_mid(chunks, CH), -float(P),
                                              ends(SRC, 0, CH), ALU.mult, ALU.add))
                if tile is None:
                    link(eng.scalar_tensor_tensor(k.by_dst[:, SRC, :, CH:], bcast_last(chunks, DIAG - 1), -float(P),
                                                  ends(SRC, CH, SLOTS), ALU.mult, ALU.add))
                link(eng.scalar_tensor_tensor(k.by_dst[:, DST, :, :], bcast_last(chunks, SLOTS), -float(P),
                                              ends(DST, 0, SLOTS), ALU.mult, ALU.add))
                if tile is not None:
                    link(eng.memset(k.by_dst[:, :, :, CH:], -1.0))
                for w in (SRC, DST):
                    link(eng.tensor_copy(k.by_src[:, w, :, 0:CH], k.by_dst[:, w, :, 0:CH].rearrange("p j i -> p i j")))
                    link(eng.tensor_copy(k.by_src[:, w, :, CH:], k.by_dst[:, w, :, CH:]))


def in_rounds(nc, k, one_round):
    with nc.Fori(0, k.n_rounds) as rnd:
        one_round(rnd)
        with nc.If(k.n_rounds > 1):
            with nc.If(rnd + 1 < k.n_rounds):
                tiles_phase(nc, k, MAIN + rnd)
            with nc.Else():
                tiles_phase(nc, k, None)


def done(row, b):
    return row * NB + (NB + b + 1)


def staged(eng, *stages):
    def steps(row, before, last=NB):
        for b in range(last):
            for lag, f in stages:
                if b >= lag:
                    if last == NB:
                        f(row, b - lag)
                elif before is not None:
                    f(before, b - lag + NB)

    steps(0, None)
    with eng.Fori(1, CH) as row:
        steps(row, row - 1)
    steps(None, CH - 1, max(lag for lag, _ in stages))


def buffers(n):
    use = [b % n for b in range(NB)]
    if n > 2 and NB % n == 1:
        use[-1] = 1
    back = [next(d for d in range(1, 2 * NB) if use[(b - d) % NB] == use[b]) for b in range(NB)]
    return use, back


def chunk_of(row, b, j):
    s = b * BT + j
    return bass.ds(s, 1) if s < CH else bass.ds(row, 1)


def flat(ap):
    return ap.rearrange("p a b -> p (a b)")


def sum_phase(nc, k, name, frm, to, ends, table, width):
    with Phase(nc, name) as ph:
        N_HOT, N_COUNTS, N_BANKS = 5, 5, 4
        hot = [ph.sb(f"hot{i}", [P, 2, BT, P], BF16) for i in range(N_HOT)]
        counts = [ph.sb(f"counts{i}", [P, BT, P], BF16) for i in range(N_COUNTS)]
        psA = [ph.ps(f"psA{i}", [P, BT * P], F32) for i in range(N_BANKS)]
        acc = ph.ps("acc", [P, 512], F32)
        hot_ready, counted_, copied = ph.sem("hot_ready"), ph.sem("counted", NB), ph.sem("copied", NB)
        applied, row_read = ph.sem("applied", NB), ph.sem("row_read", 1)
        ph.begin()
        (hot_of, hot_back), (bank_of, bank_back) = buffers(N_HOT), buffers(N_BANKS)
        counts_of, counts_back = buffers(N_COUNTS)
        with nc.Block() as block:

            @block.vector
            def _(eng):
                def one_hots(row, b):
                    eng.wait_ge(counted_, done(row, b - hot_back[b]))
                    for n, w in enumerate((frm, to)):
                        eng.tensor_tensor(hot[hot_of[b]][:, n, :, :], bcast_mid(k.iota[:], BT),
                                          bcast_last(flat(ends[:, w, bass.ds(row, 1), b * BT:(b + 1) * BT]), P),
                                          ALU.is_equal).then_inc(hot_ready, 1)

                def add_row(row, b):
                    if b == NB - 1:
                        eng.wait_ge(applied, done(row, b))
                        here = flat(k.sums[:, bass.ds(row, 1), 0:width])
                        eng.tensor_tensor(here, here, acc[:, 0:width], ALU.add).then_inc(row_read, 1)

                staged(eng, (4, add_row), (0, one_hots))

            @block.scalar
            def _(eng):
                def copy(row, b):
                    eng.wait_ge(counted_, done(row, b))
                    eng.wait_ge(applied, done(row, b - counts_back[b]))
                    eng.copy(flat(counts[counts_of[b]][:]), psA[bank_of[b]][:]).then_inc(copied, 1)

                staged(eng, (1, copy))

            @block.tensor
            def _(eng):
                def count(row, b):
                    eng.wait_ge(hot_ready, row * (2 * NB) + (2 * b + 2))
                    eng.wait_ge(copied, done(row, b - bank_back[b]))
                    for j in range(BT):
                        last = eng.matmul(psA[bank_of[b]][:, j * P:(j + 1) * P], hot[hot_of[b]][:, 0, j, :],
                                          hot[hot_of[b]][:, 1, j, :], start=True, stop=True)
                    last.then_inc(counted_, 1)

                def apply(row, b):
                    eng.wait_ge(copied, done(row, b))
                    if b == 0:
                        eng.wait_ge(row_read, row + 1)
                    for j in range(BT):
                        inner = chunk_of(row, b, j)
                        for part in range(3):
                            last = eng.matmul(acc[:, 0:width], counts[counts_of[b]][:, j, :],
                                              flat(table[:, inner, part, 0:width]),
                                              start=(b == 0 and j == 0 and part == 0),
                                              stop=(b == NB - 1 and j == BT - 1 and part == 2))
                    last.then_inc(applied, 1)

                staged(eng, (0, count), (2, apply))


def max_phase(nc, k):
    with Phase(nc, "max") as ph:
        N_HOT, N_NONE, N_BANKS = 5, 5, 2
        hot = [ph.sb(f"hot{i}", [P, 2, BT, P], BF16) for i in range(N_HOT)]
        none = [ph.sb(f"none{i}", [P, BT, P], BF16) for i in range(N_NONE)]
        query, own_key = ph.sb("query", [P, H // 2, P], BF16), ph.sb("own_key", [P, H // 2, P], BF16)
        tops = ph.sb("tops", [P, SLOTS, H // 2, 2], F32)
        top = ph.sb("top", [P, H], F32)
        psA = [ph.ps(f"psA{i}", [P, BT * P], F32) for i in range(N_BANKS)]
        psS = [ph.ps(f"psS{i}", [P, H * P], F32) for i in range(4)]
        hot_ready, counted_, copied = ph.sem("hot_ready"), ph.sem("counted", NB), ph.sem("copied", NB)
        scored, read = ph.sem("scored", SLOTS), ph.sem("read", SLOTS)
        query_ready, row_done = ph.sem("query_ready"), ph.sem("row_done", 1)
        ph.begin()
        (hot_of, hot_back), (bank_of, bank_back) = buffers(N_HOT), buffers(N_BANKS)
        none_of, none_back = buffers(N_NONE)

        def tiles_done(row, b, n=0):
            return row * SLOTS + (SLOTS + b * BT + n)

        with nc.Block() as block:

            @block.vector
            def _(eng):
                def one_hots(row, b):
                    eng.wait_ge(counted_, done(row, b - hot_back[b]))
                    for n, w in enumerate((SRC, DST)):
                        eng.tensor_tensor(hot[hot_of[b]][:, n, :, :], bcast_mid(k.iota[:], BT),
                                          bcast_last(flat(k.by_src[:, w, bass.ds(row, 1), b * BT:(b + 1) * BT]), P),
                                          ALU.is_equal).then_inc(hot_ready, 1)

                def tops_of(row, b):
                    if b == 0:
                        eng.wait_ge(row_done, 2 * row + 1)
                    for n in range(BT):
                        s, odd = b * BT + n // 2 * 2, n % 2
                        eng.wait_ge(scored, tiles_done(row, b, n + 1))
                        eng.tensor_reduce(tops[:, s:s + 2, :, odd],
                                          psS[n][:].rearrange("p (s h t) -> p s h t", s=2, h=H // 2),
                                          AX_X, ALU.max).then_inc(read, 1)
                    if b == NB - 1:
                        eng.wait_ge(read, tiles_done(row, b, BT))
                        eng.tensor_reduce(top[:], tops[:].rearrange("p s h o -> p (h o) s"), AX_X, ALU.max)\
                           .then_inc(row_done, 1)
                        eng.wait_ge(row_done, 2 * row + 2)
                        here = flat(k.peak[:, bass.ds(row, 1), :])
                        eng.tensor_tensor(here, here, top[:], ALU.max).then_inc(row_done, 1)

                staged(eng, (0, one_hots), (3, tops_of))

            @block.scalar
            def _(eng):
                def copy(row, b):
                    if b == 0:
                        eng.wait_ge(scored, tiles_done(row, 0))
                        for own, table in ((query, k.qt), (own_key, k.kt)):
                            eng.copy(flat(own[:]), table[:, bass.ds(row, 1), :, :].rearrange("p a b c -> p (a b c)"))\
                               .then_inc(query_ready, 1)
                    eng.wait_ge(counted_, done(row, b))
                    eng.wait_ge(scored, tiles_done(row, b - none_back[b] + 1))
                    eng.activation(flat(none[none_of[b]][:]), psA[bank_of[b]][:], ACT.Relu, bias=1.0,
                                   scale=-1.0).then_inc(copied, 1)

                staged(eng, (1, copy))

            @block.tensor
            def _(eng):
                def count(row, b):
                    eng.wait_ge(hot_ready, row * (2 * NB) + (2 * b + 2))
                    eng.wait_ge(copied, done(row, b - bank_back[b]))
                    for j in range(BT):
                        last = eng.matmul(psA[bank_of[b]][:, j * P:(j + 1) * P], hot[hot_of[b]][:, 0, j, :],
                                          hot[hot_of[b]][:, 1, j, :], start=True, stop=True)
                    last.then_inc(counted_, 1)

                def score(row, b):
                    eng.wait_ge(copied, done(row, b))
                    if b == 0:
                        eng.wait_ge(query_ready, 2 * row + 2)
                    for n in range(BT):
                        first, odd = n // 2 * 2, n % 2
                        eng.wait_ge(read, tiles_done(row, b - 1, n + 1))
                        eng.matmul(psS[n][:].rearrange("p (s h t) -> p s h t", s=2, h=H // 2), k.neg_ident[:],
                                   none[none_of[b]][:, first:first + 2, :].unsqueeze(2)
                                   .to_broadcast([P, 2, H // 2, P]), start=True, stop=False)
                        rows = slice(64 * odd, 64 * odd + QS)
                        for m in range(4):
                            s, pair = b * BT + first + m // 2, m % 2
                            key = k.kt[rows, s, pair, :] if s < CH else own_key[rows, pair, :]
                            last = eng.matmul(psS[n][:, m * P:(m + 1) * P], query[rows, pair, :], key,
                                              start=False, stop=(m == 3))
                        last.then_inc(scored, 1)

                staged(eng, (0, count), (2, score))


def gather_weights(eng, hot, psT, ident, signal):
    for j in range(BT):
        last = eng.transpose(psT[:, j * P:(j + 1) * P], hot[:, j, :], ident[:])
    last.then_inc(signal, 1)


def attend_phase(nc, k):
    (long_of, long_back), (msg_of, msg_back) = buffers(7), buffers(5)
    (three, back3), (two, back2) = buffers(3), buffers(2)
    with Phase(nc, "attend") as ph:
        hot_src = [ph.sb(f"hot_src{i}", [P, BT, P], F32) for i in range(7)]
        hot_dst = [ph.sb(f"hot_dst{i}", [P, BT, P], BF16) for i in range(3)]
        sel_src = [ph.sb(f"sel_src{i}", [P, BT, P], BF16) for i in range(3)]
        sel_dst = [ph.sb(f"sel_dst{i}", [P, BT, P], BF16) for i in range(3)]
        query = [ph.sb(f"query{i}", [P, BT, H * DH + H], F32) for i in range(3)]
        prod = [ph.sb(f"prod{i}", [P, BT, H * DH], F32) for i in range(3)]
        logit = [ph.sb(f"logit{i}", [P, 2, BT, H], F32) for i in range(3)]
        msg = [ph.sb(f"msg{i}", [P, BT, D + H], F32) for i in range(5)]
        psTs, psTd = ph.ps("psTs", [P, BT * P], F32), ph.ps("psTd", [P, BT * P], BF16)
        psQ = [ph.ps(f"psQ{i}", [P, 512], F32) for i in range(2)]
        psK = [ph.ps(f"psK{i}", [P, 512], F32) for i in range(3)]
        acc = ph.ps("acc", [P, 512], F32)
        hot_ready, turned, copied = ph.sem("hot_ready"), ph.sem("turned", NB), ph.sem("copied", NB)
        gathered, chain, weighed = ph.sem("gathered", NB), ph.sem("chain"), ph.sem("weighed", NB)
        msg_ready, scattered = ph.sem("msg_ready", NB), ph.sem("scattered", NB)
        row_read, logits, query_ready = ph.sem("row_read", 1), ph.sem("logits", NB), ph.sem("query_ready", NB)
        ph.begin()
        QW, KW = H * DH + H, H * DH + D

        with nc.Block() as block:

            @block.vector
            def _(eng):
                def start(row, b):
                    eng.wait_ge(scattered, done(row, b - long_back[b]))
                    eng.wait_ge(turned, done(row, b - back3[b]))
                    for h, w in ((hot_src[long_of[b]], SRC), (hot_dst[three[b]], DST)):
                        eng.tensor_tensor(h[:], bcast_mid(k.iota[:], BT),
                                          bcast_last(flat(k.by_src[:, w, bass.ds(row, 1), b * BT:(b + 1) * BT]), P),
                                          ALU.is_equal).then_inc(hot_ready, 1)

                def score(row, b):
                    q = query[three[b]]
                    kv = psK[three[b]][:, 0:BT * KW].rearrange("p (t c) -> p t c", c=KW)
                    eng.wait_ge(query_ready, done(row, b))
                    eng.wait_ge(weighed, done(row, b - back3[b]))
                    eng.tensor_tensor(prod[three[b]][:], q[:, :, 0:H * DH], kv[:, :, 0:H * DH], ALU.mult)\
                       .then_inc(chain, 1)
                    eng.wait_ge(chain, row * (2 * NB) + (2 * b + 1))
                    eng.tensor_reduce(flat(logit[three[b]][:, 0, :, :]),
                                      flat(prod[three[b]][:]).rearrange("p (s d) -> p s d", d=DH),
                                      AX_X, ALU.add).then_inc(chain, 1)
                    eng.wait_ge(chain, row * (2 * NB) + (2 * b + 2))
                    eng.tensor_tensor(logit[three[b]][:, 1, :, :], logit[three[b]][:, 0, :, :], q[:, :, H * DH:],
                                      ALU.subtract).then_inc(logits, 1)

                def message(row, b):
                    kv = psK[three[b]][:, 0:BT * KW].rearrange("p (t c) -> p t c", c=KW)
                    m = msg[msg_of[b]]
                    eng.wait_ge(weighed, done(row, b))
                    for j in range(BT):
                        last = eng.tensor_tensor(m[:, j, 0:D].rearrange("p (h v) -> p h v", h=H),
                                                 kv[:, j, H * DH:].rearrange("p (h v) -> p h v", h=H),
                                                 bcast_last(m[:, j, D:], DV), ALU.mult)
                    last.then_inc(msg_ready, 1)

                def add_row(row, b):
                    if b == NB - 1:
                        eng.wait_ge(scattered, done(row, b))
                        here = flat(k.sums[:, bass.ds(row, 1), 0:D + H])
                        eng.tensor_tensor(here, here, acc[:, 0:D + H], ALU.add).then_inc(row_read, 1)

                staged(eng, (0, start), (3, score), (4, message), (6, add_row))

            @block.scalar
            def _(eng):
                def copy(row, b):
                    eng.wait_ge(turned, done(row, b))
                    eng.wait_ge(gathered, done(row, b - back3[b]))
                    eng.copy(flat(sel_src[three[b]][:]), psTs[:])
                    eng.copy(flat(sel_dst[three[b]][:]), psTd[:]).then_inc(copied, 1)

                def weigh(row, b):
                    eng.wait_ge(logits, done(row, b))
                    eng.wait_ge(scattered, done(row, b - msg_back[b]))
                    eng.activation(msg[msg_of[b]][:, :, D:], logit[three[b]][:, 1, :, :], ACT.Exp)\
                       .then_inc(weighed, 1)

                def copy_query(row, b):
                    eng.wait_ge(gathered, done(row, b))
                    eng.wait_ge(logits, done(row, b - back3[b]))
                    eng.copy(flat(query[three[b]][:]), psQ[two[b]][:, 0:BT * QW]).then_inc(query_ready, 1)

                staged(eng, (1, copy), (2, copy_query), (3, weigh))

            @block.tensor
            def _(eng):
                def turn(row, b):
                    eng.wait_ge(hot_ready, row * (2 * NB) + (2 * b + 2))
                    eng.wait_ge(copied, done(row, b - 1))
                    for j in range(BT):
                        eng.transpose(psTs[:, j * P:(j + 1) * P], hot_src[long_of[b]][:, j, :], k.ident[:])
                    gather_weights(eng, hot_dst[three[b]], psTd, k.identb, turned)

                def gather(row, b):
                    eng.wait_ge(copied, done(row, b))
                    eng.wait_ge(query_ready, done(row, b - back2[b]))
                    eng.wait_ge(msg_ready, done(row, b - back3[b]))
                    for j in range(BT):
                        for part in range(3):
                            eng.matmul(psQ[two[b]][:, j * QW:(j + 1) * QW], sel_src[three[b]][:, j, :],
                                       flat(k.qm[:, bass.ds(row, 1), part, :]), start=(part == 0), stop=(part == 2))
                        for part in range(3):
                            last = eng.matmul(psK[three[b]][:, j * KW:(j + 1) * KW], sel_dst[three[b]][:, j, :],
                                              flat(k.kv[:, chunk_of(row, b, j), part, :]),
                                              start=(part == 0), stop=(part == 2))
                    last.then_inc(gathered, 1)

                def scatter(row, b):
                    eng.wait_ge(msg_ready, done(row, b))
                    if b == 0:
                        eng.wait_ge(row_read, row + 1)
                    for j in range(BT):
                        last = eng.matmul(acc[:, 0:D + H], hot_src[long_of[b]][:, j, :], msg[msg_of[b]][:, j, :],
                                          start=(b == 0 and j == 0), stop=(b == NB - 1 and j == BT - 1))
                    last.then_inc(scattered, 1)

                staged(eng, (1, turn), (2, gather), (5, scatter))


HALVES = ((0, 7 * BT), (7 * BT, SLOTS))


def message_phase(nc, k, rnd):
    (long_of, long_back), (msg_of, msg_back) = buffers(7), buffers(5)
    (three, back3), (two, back2) = buffers(3), buffers(2)
    with Phase(nc, "message") as ph:
        hot_dst = [ph.sb(f"hot_dst{i}", [P, BT, P], F32) for i in range(7)]
        hot_src = [ph.sb(f"hot_src{i}", [P, BT, P], BF16) for i in range(3)]
        sel_src = [ph.sb(f"sel_src{i}", [P, BT, P], BF16) for i in range(3)]
        edge = [ph.sb(f"edge{i}", [P, b - a, D], F32) for i, (a, b) in enumerate(HALVES)]
        raw = [ph.sb(f"raw{i}", [P, BT, D], F32) for i in range(3)]
        msg = [ph.sb(f"msg{i}", [P, BT, D], F32) for i in range(5)]
        psT = [ph.ps(f"psT{i}", [P, BT * P], BF16) for i in range(2)]
        psG = [ph.ps(f"psG{i}", [P, 512], F32) for i in range(3)]
        acc = ph.ps("acc", [P, 512], F32)
        hot_ready, turned, copied = ph.sem("hot_ready"), ph.sem("turned", NB), ph.sem("copied", NB)
        gathered, added, made = ph.sem("gathered", NB), ph.sem("added", NB), ph.sem("made", NB)
        scattered, row_read = ph.sem("scattered", NB), ph.sem("row_read", 1)
        here_in = [ph.sem(f"here_in{i}") for i in range(2)]
        ph.begin()
        rows = k.edge_rows.rearrange("(p t) d -> p t d", p=P)
        with nc.Block() as block:

            @block.sync
            def _(eng):
                with eng.Fori(0, CH) as row:
                    for n, (a, b) in enumerate(HALVES):
                        with eng.If(rnd < 1):
                            eng.wait_ge(added, done(row, b // BT - 1 - NB))
                            eng.dma_start(edge[n][:], rows[:, bass.ds(row * SLOTS + a, b - a), :])\
                               .then_inc(here_in[n], 16)
                        with eng.Else():
                            eng.wait_ge(added, done(row, b // BT - 1 - NB))
                            eng.dma_start(edge[n][:], rows[:, bass.ds(MAIN - 1 + rnd, 1), :]
                                          .to_broadcast([P, b - a, D])).then_inc(here_in[n], 16)

            @block.vector
            def _(eng):
                def start(row, b):
                    eng.wait_ge(scattered, done(row, b - long_back[b]))
                    eng.wait_ge(turned, done(row, b - back3[b]))
                    for h, w in ((hot_src[three[b]], SRC), (hot_dst[long_of[b]], DST)):
                        eng.tensor_tensor(h[:], bcast_mid(k.iota[:], BT),
                                          bcast_last(flat(k.by_dst[:, w, bass.ds(row, 1), b * BT:(b + 1) * BT]), P),
                                          ALU.is_equal).then_inc(hot_ready, 1)

                def add(row, b):
                    eng.wait_ge(gathered, done(row, b))
                    eng.wait_ge(made, done(row, b - back3[b]))
                    half = int(b * BT >= HALVES[0][1])
                    first, last = (HALVES[half][n] for n in (0, 1))
                    if b * BT == first:
                        eng.wait_ge(here_in[half], row * 16 + 16)
                    s = b * BT - first
                    eng.tensor_tensor(flat(raw[three[b]][:]), psG[three[b]][:, 0:BT * D],
                                      flat(edge[half][:, s:s + BT, :]), ALU.add).then_inc(added, 1)

                def add_row(row, b):
                    if b == NB - 1:
                        eng.wait_ge(scattered, done(row, b))
                        here = flat(k.sums[:, bass.ds(row, 1), 0:D])
                        eng.tensor_tensor(here, here, acc[:, 0:D], ALU.add).then_inc(row_read, 1)

                staged(eng, (4, add), (0, start), (6, add_row))

            @block.scalar
            def _(eng):
                def copy(row, b):
                    eng.wait_ge(turned, done(row, b))
                    eng.wait_ge(gathered, done(row, b - back3[b]))
                    eng.copy(flat(sel_src[three[b]][:]), psT[two[b]][:]).then_inc(copied, 1)

                def rectify(row, b):
                    eng.wait_ge(added, done(row, b))
                    eng.wait_ge(scattered, done(row, b - msg_back[b]))
                    eng.activation(flat(msg[msg_of[b]][:]), flat(raw[three[b]][:]), ACT.Relu).then_inc(made, 1)

                staged(eng, (1, copy), (4, rectify))

            @block.tensor
            def _(eng):
                def turn(row, b):
                    eng.wait_ge(hot_ready, row * (2 * NB) + (2 * b + 2))
                    eng.wait_ge(copied, done(row, b - back2[b]))
                    gather_weights(eng, hot_src[three[b]], psT[two[b]], k.identb, turned)

                def gather(row, b):
                    eng.wait_ge(copied, done(row, b))
                    eng.wait_ge(added, done(row, b - back3[b]))
                    for j in range(BT):
                        for part in range(3):
                            last = eng.matmul(psG[three[b]][:, j * D:(j + 1) * D], sel_src[three[b]][:, j, :],
                                              flat(k.table[:, chunk_of(row, b, j), part, :]),
                                              start=(part == 0), stop=(part == 2))
                    last.then_inc(gathered, 1)

                def scatter(row, b):
                    eng.wait_ge(made, done(row, b))
                    if b == 0:
                        eng.wait_ge(row_read, row + 1)
                    for j in range(BT):
                        last = eng.matmul(acc[:, 0:D], hot_dst[long_of[b]][:, j, :], msg[msg_of[b]][:, j, :],
                                          start=(b == 0 and j == 0), stop=(b == NB - 1 and j == BT - 1))
                    last.then_inc(scattered, 1)

                staged(eng, (1, turn), (2, gather), (5, scatter))


DENSE = 7
assert CH % DENSE == 0


def dense_phase(nc, k, name, rows, weight, width, result, bias=None):
    with Phase(nc, name) as ph:
        staged_rows = ph.sb("staged_rows", [P, DENSE, D], F32)
        turned_rows = ph.sb("turned_rows", [D, DENSE, P], F32)
        staged, turning = ph.sem("staged"), ph.sem("turning")
        psT = ph.ps("psT", [D, 8 * P], F32)
        psY = ph.ps("psY", [P, 8 * P], F32)
        turned, copied = ph.sem("turned"), ph.sem("copied")
        multiplied, written = ph.sem("multiplied", 1), ph.sem("written", 1)
        ph.begin()
        with nc.Block() as block:

            @block.tensor
            def _(eng):
                with eng.Fori(0, CH // DENSE) as g:
                    eng.wait_ge(staged, g + 1)
                    eng.sem_inc(turning, 1)
                    for c in range(DENSE):
                        last = eng.transpose(psT[:, c * P:(c + 1) * P], staged_rows[:, c, :], k.ident[:])
                    last.then_inc(turned, 1)
                    eng.wait_ge(copied, g + 1)
                    eng.wait_ge(written, g + 1)
                    for c in range(DENSE):
                        last = eng.matmul(psY[:, c * P:c * P + width], turned_rows[:, c, :], weight[:],
                                          start=True, stop=True)
                    last.then_inc(multiplied, 1)

            @block.scalar
            def _(eng):
                with eng.Fori(0, CH // DENSE) as g:
                    eng.wait_ge(multiplied, g + 1)
                    eng.copy(staged_rows[:], rows[:, bass.ds(g * DENSE, DENSE), :]).then_inc(staged, 1)
                    eng.wait_ge(turned, g + 1)
                    eng.copy(flat(turned_rows[:]), psT[:, 0:DENSE * P]).then_inc(copied, 1)

            @block.vector
            def _(eng):
                y = psY[:, 0:DENSE * P].rearrange("p (c w) -> p c w", w=P)[:, :, 0:width]
                with eng.Fori(0, CH // DENSE) as g:
                    eng.wait_ge(multiplied, g + 2)
                    out = result[:, bass.ds(g * DENSE, DENSE), 0:width]
                    if bias is None:
                        eng.tensor_copy(out, y).then_inc(written, 1)
                    else:
                        eng.tensor_tensor(out, y, bcast_mid(bias[:, 0:width], DENSE), ALU.add).then_inc(written, 1)
                eng.wait_ge(written, CH // DENSE + 1)


def node_phase(nc, k, name, work):
    with Phase(nc, name) as ph:
        step = ph.sem("step")
        with nc.Block() as block:

            @block.vector
            def _(eng):
                work(eng, counted(eng, step))


def root_phase(nc, k, name, *rows):
    with Phase(nc, name) as ph:
        root = ph.sb("root", [P, len(rows), CH], F32)
        square = ph.sb("square", [P, len(rows), CH], F32)
        rooted, step = ph.sem("rooted"), ph.sem("step")
        with nc.Block() as block:

            @block.scalar
            def _(eng):
                for n, (row, factor) in enumerate(rows):
                    eng.activation(root[:, n, :], row, ACT.Sqrt).then_inc(rooted, 1)

            @block.vector
            def _(eng):
                link = counted(eng, step)
                eng.wait_ge(rooted, len(rows))
                link(eng.reciprocal(root[:], root[:]))
                link(eng.tensor_tensor(square[:], root[:], root[:], ALU.mult))
                for n, (row, factor) in enumerate(rows):
                    link(eng.tensor_tensor(square[:, n, :], square[:, n, :], row, ALU.mult))
                link(eng.tensor_scalar(square[:], square[:], -0.5, 1.5, ALU.mult, ALU.add))
                for n, (row, factor) in enumerate(rows):
                    link(eng.scalar_tensor_tensor(row, root[:, n, :], factor, square[:, n, :], ALU.mult, ALU.mult))


def norm_stats(eng, link, k):
    mean, var = k.stat[:, 0, :], k.stat[:, 1, :]
    centred, square = k.wide[:, :, 0:D], k.wide[:, :, D:2 * D]
    link(eng.tensor_reduce(mean, k.X[:], AX_X, ALU.add))
    link(eng.tensor_single_scalar(mean, mean, 1.0 / D, ALU.mult))
    link(eng.tensor_tensor(centred, k.X[:], bcast_last(mean, D), ALU.subtract))
    link(eng.tensor_tensor(square, centred, centred, ALU.mult))
    link(eng.tensor_reduce(var, square, AX_X, ALU.add))
    link(eng.tensor_scalar(var, var, 1.0 / D, 1e-5, ALU.mult, ALU.add))


def norm_relu(eng, link, k):
    link(eng.tensor_tensor(k.hidden[:], k.wide[:, :, 0:D], bcast_last(k.stat[:, 1, :], D), ALU.mult))
    link(eng.tensor_single_scalar(k.hidden[:], k.hidden[:], 0.0, ALU.max))


def split(eng, link, value, parts, rest):
    left = value
    for n, copies in enumerate(parts):
        for c in copies:
            link(eng.tensor_copy(c, left))
        if n < 2:
            link(eng.tensor_tensor(rest, left, copies[0], ALU.subtract))
            left = rest


def split_table(eng, link, k, value, width):
    split(eng, link, value, [[k.table[:, :, n, 0:width]] for n in range(3)], k.rest[:, :, 0:width])



def stacked_phase(nc, k, name, value, places, turned):
    with Phase(nc, name) as ph:
        stack = ph.sb("stack", [P, CH, H, 64], BF16)
        staged_rows = ph.sb("staged_rows", [P, DENSE, H, 64], BF16)
        staged = ph.sem("staged")
        rest = ph.sb("rest", [P, CH, H * DH], F32)
        psT = ph.ps("psT", [P, DENSE * 2 * P], BF16)
        step, turned_, copied = ph.sem("step"), ph.sem("turned"), ph.sem("copied")
        with nc.Block() as block:

            @block.vector
            def _(eng):
                link = counted(eng, step)
                link(eng.memset(stack[:], 0.0))
                heads = value.rearrange("p c (h d) -> p c h d", h=H)
                left = rest[:].rearrange("p c (h d) -> p c h d", h=H)
                for h in range(H):
                    split(eng, link, heads[:, :, h, :],
                          [[stack[:, :, h, DH * i:DH * (i + 1)] for i in where] for where in places],
                          left[:, :, h, :])

            @block.tensor
            def _(eng):
                with eng.Fori(0, CH // DENSE) as g:
                    eng.wait_ge(staged, g + 1)
                    for c in range(DENSE):
                        for pair in range(H // 2):
                            at = (2 * c + pair) * P
                            last = eng.transpose(psT[:, at:at + P],
                                                 flat(staged_rows[:, c, 2 * pair:2 * pair + 2, :]), k.identb[:])
                    last.then_inc(turned_, 1)

            @block.scalar
            def _(eng):
                eng.wait_ge(step, STACK_STEPS)
                with eng.Fori(0, CH // DENSE) as g:
                    eng.copy(staged_rows[:], stack[:, bass.ds(g * DENSE, DENSE), :, :]).then_inc(staged, 1)
                    eng.wait_ge(turned_, g + 1)
                    eng.copy(turned[:, bass.ds(g * DENSE, DENSE), :, :].rearrange("p a b c -> p (a b c)"), psT[:])\
                       .then_inc(copied, 1)


STACK_STEPS = 1 + H * (PARTS + 2)


def store_phase(nc, k):
    with Phase(nc, "store") as ph:
        stored = ph.sem("stored")
        with nc.Block() as block:

            @block.sync
            def _(eng):
                eng.dma_start(k.out[0:(CH - 1) * P, :].rearrange("(c p) d -> p c d", p=P), k.X[:, 0:CH - 1, :])\
                   .then_inc(stored, 16)
                eng.dma_start(k.out[(CH - 1) * P:N_NODES, :], k.X[0:TAIL, CH - 1, :]).then_inc(stored, 16)
                eng.wait_ge(stored, 32)


def program(nc, dram, out):
    k = Kernel()
    k.x, k.src, k.dst, k.edge_attr = (dram[n] for n in ("x", "src", "dst", "edge_attr_64"))
    k.out = out
    k.edge_meta = nc.dram_tensor("edge_meta", (P * NT, 2), F32, kind="Internal").ap()
    k.edge_rows = nc.dram_tensor("edge_rows", (P * NT, D), F32, kind="Internal").ap()
    with ExitStack() as ctx:
        def sb(name, shape, dt):
            return ctx.enter_context(nc.sbuf_tensor(name, shape, dt))

        k.sent = [ctx.enter_context(nc.semaphore(f"sent{i}")) for i in range(2)]
        k.X = sb("X", [P, CH, D], F32)
        k.ident, k.identb = sb("ident", [P, P], F32), sb("identb", [P, P], BF16)
        k.neg_ident = sb("neg_ident", [P, P], BF16)
        k.later = sb("later", [P, EP], F32)
        k.iota = sb("iota", [P, P], BF16)
        k.slot_row = sb("slot_row", [P, 1], F32)
        k.deg = sb("deg", [P, 2, CH], F32)
        k.rounds = sb("rounds", [1, 1], I32)
        k.sums = sb("sums", [P, CH, D + H], F32)
        k.hidden = sb("hidden", [P, CH, D], F32)
        k.wide = sb("wide", [P, CH, 2 * D], F32)
        k.stat = sb("stat", [P, 6, CH], F32)
        weight = {n: sb(n, list(dram[n].shape), F32) for n in dram if "_W" in n}
        bias = {n: sb(n, [P, dram[n].shape[0]], F32) for n in dram if "_b" in n}
        k.weights = [(weight[n][:], dram[n]) for n in weight]
        k.weights += [(bias[n][:], dram[n].rearrange("(a n) -> a n", a=1).to_broadcast([P, dram[n].shape[0]]))
                      for n in bias]
        setup_phase(nc, k)
        place_phase(nc, k)
        k.n_rounds = nc.values_load(k.rounds[0:1, 0:1], min_val=1, max_val=ET + 1)
        k.by_dst = sb("by_dst", [P, 2, CH, SLOTS], F32)
        k.by_src = sb("by_src", [P, 2, CH, SLOTS], F32)
        tiles_phase(nc, k, None)
        sums, hidden, wide = k.sums, k.hidden, k.wide
        rows_of = sums[:, :, 0:D]
        dinv = k.stat[:, 3, :]
        tables = ExitStack()

        def table(width):
            k.table = tables.enter_context(nc.sbuf_tensor(f"table{nc.next_id()}", [P, CH, 3, width], BF16))
            k.rest = tables.enter_context(nc.sbuf_tensor(f"rest{nc.next_id()}", [P, CH, width], F32))

        table(D + 1)

        def first(eng, link):
            link(eng.tensor_single_scalar(dinv, k.deg[:, DST, :], 1.0, ALU.add))
            norm_stats(eng, link, k)

        def scaled(eng, link):
            link(eng.tensor_tensor(wide[:, :, 0:D], wide[:, :, 0:D], bcast_last(dinv, D), ALU.mult))
            split_table(eng, link, k, wide[:, :, 0:D], D)
            link(eng.memset(sums[:], 0.0))

        def convolved(b):
            def work(eng, link):
                link(eng.tensor_tensor(rows_of, rows_of, wide[:, :, 0:D], ALU.add))
                link(eng.tensor_tensor(rows_of, rows_of, bcast_last(dinv, D), ALU.mult))
                link(eng.tensor_tensor(rows_of, rows_of, bcast_mid(b[:], CH), ALU.add))
                link(eng.tensor_single_scalar(hidden[:], rows_of, 0.0, ALU.max))
            return work

        var = k.stat[:, 1, :]
        node_phase(nc, k, "stats0", first)
        root_phase(nc, k, "root0", (dinv, 1.0), (var, 1.0))
        node_phase(nc, k, "norm0", lambda eng, link: norm_relu(eng, link, k))
        for n in (1, 2):
            dense_phase(nc, k, f"conv{n}_dense", hidden, weight[f"L0_gnn_W{n}"], D, wide)
            node_phase(nc, k, f"conv{n}_table", scaled)
            in_rounds(nc, k, lambda rnd: sum_phase(nc, k, f"conv{n}", SRC, DST, k.by_dst, k.table, D))
            node_phase(nc, k, f"conv{n}_end", convolved(bias[f"L0_gnn_b{n}"]))

        have = k.stat[:, 4, :]

        def layer1_stats(eng, link):
            link(eng.tensor_tensor(k.X[:], k.X[:], hidden[:], ALU.add))
            norm_stats(eng, link, k)
            link(eng.tensor_single_scalar(have, k.deg[:, DST, :], 1.0, ALU.max))

        def layer1(eng, link):
            norm_relu(eng, link, k)
            link(eng.tensor_single_scalar(dinv, k.deg[:, DST, :], 0.0, ALU.is_gt))
            link(eng.tensor_tensor(dinv, dinv, have, ALU.mult))
            link(eng.tensor_tensor(wide[:, :, 0:D], hidden[:], bcast_last(dinv, D), ALU.mult))
            link(eng.tensor_copy(wide[:, :, D], dinv))
            split_table(eng, link, k, wide[:, :, 0:D + 1], D + 1)
            link(eng.memset(sums[:], 0.0))

        def layer1_sums(eng, link):
            link(eng.tensor_tensor(sums[:, :, 0:D + 1], sums[:, :, 0:D + 1], bcast_last(dinv, D + 1), ALU.mult))
            link(eng.tensor_tensor(hidden[:], hidden[:], rows_of, ALU.mult))
            link(eng.tensor_tensor(bias["L1_gnn_b1"][:], bias["L1_gnn_b1"][:], bias["L1_gnn_b2"][:], ALU.add))

        def layer1_end(eng, link):
            link(eng.tensor_tensor(rows_of, wide[:, :, 0:D], wide[:, :, D:], ALU.add))
            link(eng.tensor_tensor(hidden[:], bcast_last(sums[:, :, D], D), bcast_mid(bias["L1_gnn_b1"][:], CH),
                                   ALU.mult))
            link(eng.tensor_tensor(rows_of, rows_of, hidden[:], ALU.add))
            link(eng.scalar_tensor_tensor(hidden[:], rows_of, 0.2, rows_of, ALU.mult, ALU.max))
            link(eng.tensor_tensor(k.X[:], k.X[:], hidden[:], ALU.add))

        node_phase(nc, k, "layer1_stats", layer1_stats)
        root_phase(nc, k, "root1", (have, 1.0), (var, 1.0))
        node_phase(nc, k, "layer1_table", layer1)
        in_rounds(nc, k, lambda rnd: sum_phase(nc, k, "layer1", DST, SRC, k.by_src, k.table, D + 1))
        tables.close()
        node_phase(nc, k, "layer1_sums", layer1_sums)
        dense_phase(nc, k, "layer1_dense1", rows_of, weight["L1_gnn_W1"], D, wide)
        dense_phase(nc, k, "layer1_dense2", hidden, weight["L1_gnn_W2"], D, wide[:, :, D:])
        node_phase(nc, k, "layer1_end", layer1_end)

        def layer2_stats(eng, link):
            norm_stats(eng, link, k)
            link(eng.tensor_single_scalar(have, k.deg[:, SRC, :], 1.0, ALU.max))

        def queries(eng, link):
            link(eng.tensor_tensor(wide[:, :, 0:H * DH], wide[:, :, 0:H * DH], bcast_last(have, H * DH), ALU.mult))
            link(eng.memset(k.peak[:], -BIG))

        node_phase(nc, k, "layer2_stats", layer2_stats)
        root_phase(nc, k, "root2", (have, QK_SCALE), (var, 1.0))
        node_phase(nc, k, "norm2", lambda eng, link: norm_relu(eng, link, k))
        dense_phase(nc, k, "qkv", hidden, weight["L2_gnn_W_qkv"], 2 * D, wide, bias["L2_gnn_b_qkv"])
        k.peak = sb("peak", [P, CH, H], F32)
        node_phase(nc, k, "queries", queries)
        with nc.sbuf_tensor("qt", [P, CH, H // 2, P], BF16) as k.qt, \
                nc.sbuf_tensor("kt", [P, CH, H // 2, P], BF16) as k.kt:
            stacked_phase(nc, k, "stack_q", wide[:, :, 0:H * DH], ((0, 1, 4), (2, 3), (5,)), k.qt)
            stacked_phase(nc, k, "stack_k", wide[:, :, H * DH:2 * H * DH], ((0, 2, 5), (1, 3), (4,)), k.kt)
            in_rounds(nc, k, lambda rnd: max_phase(nc, k))
        with nc.sbuf_tensor("qm", [P, CH, 3, H * DH + H], BF16) as k.qm, \
                nc.sbuf_tensor("kv", [P, CH, 3, H * DH + D], BF16) as k.kv:
            with nc.sbuf_tensor("rest2", [P, CH, H * DH + D], F32) as rest:
                def attention_tables(eng, link):
                    q, kv = wide[:, :, 0:H * DH], wide[:, :, H * DH:]
                    split(eng, link, q, [[k.qm[:, :, n, 0:H * DH]] for n in range(3)], rest[:, :, 0:H * DH])
                    split(eng, link, k.peak[:], [[k.qm[:, :, n, H * DH:]] for n in range(3)], rest[:, :, 0:H])
                    split(eng, link, kv, [[k.kv[:, :, n, :]] for n in range(3)], rest[:])
                    link(eng.memset(sums[:], 0.0))

                node_phase(nc, k, "attention_tables", attention_tables)
            in_rounds(nc, k, lambda rnd: attend_phase(nc, k))

        def layer3(eng, link):
            link(eng.tensor_single_scalar(sums[:, :, D:], sums[:, :, D:], 1e-16, ALU.add))
            link(eng.reciprocal(sums[:, :, D:], sums[:, :, D:]))
            for h in range(H):
                link(eng.tensor_tensor(hidden[:, :, h * DV:(h + 1) * DV], sums[:, :, h * DV:(h + 1) * DV],
                                       bcast_last(sums[:, :, D + h], DV), ALU.mult))
            link(eng.tensor_tensor(k.X[:], k.X[:], hidden[:], ALU.add))
            norm_stats(eng, link, k)

        def layer3_table(eng, link):
            norm_relu(eng, link, k)
            split_table(eng, link, k, hidden[:], D)
            link(eng.memset(sums[:], 0.0))

        table(D)
        node_phase(nc, k, "layer3_stats", layer3)
        root_phase(nc, k, "root3", (var, 1.0))
        node_phase(nc, k, "layer3_table", layer3_table)
        in_rounds(nc, k, lambda rnd: message_phase(nc, k, rnd))
        tables.close()
        node_phase(nc, k, "layer3_sum", lambda eng, link:
                   link(eng.tensor_tensor(hidden[:], hidden[:], rows_of, ALU.add)))
        for n in (1, 2, 3):
            dense_phase(nc, k, f"layer3_dense{n}", hidden, weight[f"L3_gnn_W{n}"], D, wide, bias[f"L3_gnn_b{n}"])
            if n < 3:
                node_phase(nc, k, f"layer3_relu{n}", lambda eng, link:
                           link(eng.tensor_single_scalar(hidden[:], wide[:, :, 0:D], 0.0, ALU.max)))
        node_phase(nc, k, "layer3_end", lambda eng, link:
                   link(eng.tensor_tensor(k.X[:], k.X[:], wide[:, :, 0:D], ALU.add)))
        store_phase(nc, k)


def kernel(**inputs):
    import numpy as np
    import concourse.bacc as bacc
    from concourse.bass_utils import run_bass_kernel_spmd as run

    nc = bacc.Bacc("TRN2", target_bir_lowering=False, num_devices=1)
    laid = {n: np.ascontiguousarray(a.T if n[:2] in ("L1", "L3") and a.ndim == 2 else a)
            for n, a in ((n, np.asarray(a)) for n, a in inputs.items())}
    dram = {n: nc.dram_tensor(f"in_{n}", a.shape, mybir.dt.from_np(a.dtype), kind="ExternalInput").ap()
            for n, a in laid.items()}
    out = nc.dram_tensor("out", (N_NODES, D), F32, kind="ExternalOutput").ap()
    program(nc, dram, out)
    r = run(nc, [{f"in_{n}": a for n, a in laid.items()}], core_ids=[0])
    return r.results[0]["out"]
```
